# Optimizing a Trainium2 kernel written in Bass

```python
import numpy as np
import jax
import jax.numpy as jnp

def _softmax(x, axis=-1):
    return jax.nn.softmax(x, axis=axis)

def _gelu(x):
    return jax.nn.gelu(x, approximate=True)

def _silu(x):
    return jax.nn.silu(x)

def _sigmoid(x):
    return jax.nn.sigmoid(x)

def _layernorm(x, axis=-1, eps=1e-05):
    m = jnp.mean(x, axis=axis, keepdims=True)
    v = jnp.var(x, axis=axis, keepdims=True)
    return (x - m) / jnp.sqrt(v + eps)

def _scatter_add(tgt, idx, src, axis=0):
    return tgt.at[idx].add(src)

def _segment_sum(src, seg, n):
    return jax.ops.segment_sum(src, seg, n)
kernel_name = 'mk_xattn_ffn_d1_seqx_r8_6cfca1'

def setup_inputs(seed: int=0):
    np.random.seed(seed)
    _w = jnp.asarray

    def _rec_inputs():
        import jax
        import jax.numpy as jnp
        _rk = jax.random.key(seed)
        x = 7.22e-05 + 1 * jax.random.normal(jax.random.fold_in(_rk, 1), (16, 128, 256), jnp.float32)
        _lenS = 128 - jax.random.randint(jax.random.fold_in(_rk, 7), (16,), 0, max(1, 128 // 4) + 1, jnp.int32)
        _lenS2 = 128 - jax.random.randint(jax.random.fold_in(_rk, 8), (16,), 0, max(1, 128 // 4) + 1, jnp.int32)
        _ctx_2048P = jax.random.normal(jax.random.fold_in(_rk, 11), (16, 16, 256), jnp.float32)
        _ctx_2048c = jax.random.dirichlet(jax.random.fold_in(_rk, 511), 0.3 * jnp.ones((16,), jnp.float32), (16, 128))
        _ctx_2048t = jnp.einsum('bsk,bkd->bsd', _ctx_2048c, _ctx_2048P)
        _ctx_2048t = _ctx_2048t * jax.lax.rsqrt(jnp.mean(jnp.square(_ctx_2048t)) + 1e-12) * 0.953939
        ctx_2048 = 4.13588e-05 + 0.999923 * (_ctx_2048t + 0.3 * jax.random.normal(jax.random.fold_in(_rk, 611), (16, 128, 256), jnp.float32))
        return (x, ctx_2048)
    x, ctx_2048 = _rec_inputs()

    def _L0_xattn_setup():
        import jax, jax.numpy as jnp
        import numpy as np
        N_HEAD = 8
        key = jax.random.key(seed)
        k1, k2, k3 = jax.random.split(key, 3)
        B, D, L = (4, 128, 256)
        q = jax.random.normal(k1, (B, D, L), dtype=jnp.float32)
        k = jax.random.normal(k2, (B, D, L), dtype=jnp.float32)
        v = jax.random.normal(k3, (B, D, L), dtype=jnp.float32)
        gamma = jnp.ones((), dtype=jnp.float32)
        return {'q': q, 'k': k, 'v': v, 'gamma': gamma}
    _L0_xattn_all = _L0_xattn_setup()
    _L0_xattn_in = {k: v for k, v in _L0_xattn_all.items() if k in ('gamma',)}
    del _L0_xattn_all

    def _L0_ffn_setup():
        import jax, jax.numpy as jnp
        import numpy as np
        H = 256
        key = jax.random.key(seed)
        ks = jax.random.split(key, 10)
        s = 1.0 / np.sqrt(H)
        x = jax.random.normal(ks[0], (4, 256, H), dtype=jnp.float32)
        Wg = jax.random.uniform(ks[1], (2, H), jnp.float32, -s, s)
        W0a = jax.random.uniform(ks[2], (2 * H, H), jnp.float32, -s, s)
        b0a = jax.random.uniform(ks[3], (2 * H,), jnp.float32, -s, s)
        W0b = jax.random.uniform(ks[4], (H, 2 * H), jnp.float32, -s, s)
        b0b = jax.random.uniform(ks[5], (H,), jnp.float32, -s, s)
        W1a = jax.random.uniform(ks[6], (2 * H, H), jnp.float32, -s, s)
        b1a = jax.random.uniform(ks[7], (2 * H,), jnp.float32, -s, s)
        W1b = jax.random.uniform(ks[8], (H, 2 * H), jnp.float32, -s, s)
        b1b = jax.random.uniform(ks[9], (H,), jnp.float32, -s, s)
        return {'x': x, 'Wg': Wg, 'W0a': W0a, 'b0a': b0a, 'W0b': W0b, 'b0b': b0b, 'W1a': W1a, 'b1a': b1a, 'W1b': W1b, 'b1b': b1b}
    _L0_ffn_all = _L0_ffn_setup()
    _L0_ffn_in = {k: v for k, v in _L0_ffn_all.items() if k in ('Wg', 'W0a', 'b0a', 'W0b', 'b0b', 'W1a', 'b1a', 'W1b', 'b1b')}
    del _L0_ffn_all
    return {'x': x, 'ctx_2048': ctx_2048, 'L0_xattn_gamma': _L0_xattn_in['gamma'], 'L0_ffn_Wg': _L0_ffn_in['Wg'], 'L0_ffn_W0a': _L0_ffn_in['W0a'], 'L0_ffn_b0a': _L0_ffn_in['b0a'], 'L0_ffn_W0b': _L0_ffn_in['W0b'], 'L0_ffn_b0b': _L0_ffn_in['b0b'], 'L0_ffn_W1a': _L0_ffn_in['W1a'], 'L0_ffn_b1a': _L0_ffn_in['b1a'], 'L0_ffn_W1b': _L0_ffn_in['W1b'], 'L0_ffn_b1b': _L0_ffn_in['b1b']}

def reference(x, ctx_2048, L0_xattn_gamma, L0_ffn_Wg, L0_ffn_W0a, L0_ffn_b0a, L0_ffn_W0b, L0_ffn_b0b, L0_ffn_W1a, L0_ffn_b1a, L0_ffn_W1b, L0_ffn_b1b):
    import jax
    import jax.numpy as jnp

    def _L0_xattn_ref(q, k, v, gamma):
        import jax, jax.numpy as jnp
        import numpy as np
        N_HEAD = 8
        B, Dq, Lq = q.shape
        Dv, Lk = (v.shape[-2], v.shape[-1])
        h = N_HEAD
        dq = Dq // h
        dv = Dv // h
        qh = q.reshape(B, h, dq, Lq)
        kh = k.reshape(B, h, dq, Lk)
        vh = v.reshape(B, h, dv, Lk)
        scale = 1.0 / jnp.sqrt(jnp.asarray(dq, dtype=q.dtype))
        qk = jnp.einsum('bhdq,bhdl->bhql', qh, kh) * scale
        sm = jax.nn.softmax(qk, axis=-1)
        ret = jnp.einsum('bhql,bhdl->bhdq', sm, vh)
        ret = ret.reshape(B, Dv, Lq)
        return gamma * ret

    def _L0_ffn_ref(x, Wg, W0a, b0a, W0b, b0b, W1a, b1a, W1b, b1b):
        import jax, jax.numpy as jnp
        import numpy as np
        H = 256
        scores = jax.nn.softmax(jnp.einsum('bsh,eh->bse', x, Wg), axis=-1)
        top_expert = jnp.argmax(scores, axis=-1)
        h0 = jax.nn.gelu(jnp.einsum('bsh,fh->bsf', x, W0a) + b0a, approximate=False)
        out0 = jnp.einsum('bsf,hf->bsh', h0, W0b) + b0b
        h1 = jax.nn.relu(jnp.einsum('bsh,fh->bsf', x, W1a) + b1a)
        out1 = jnp.einsum('bsf,hf->bsh', h1, W1b) + b1b
        mask0 = (top_expert == 0).astype(x.dtype)[..., None]
        return out0 * mask0 + out1 * (1.0 - mask0)
    x = x + _L0_xattn_ref(_layernorm(x, axis=-1), ctx_2048, ctx_2048, L0_xattn_gamma)
    x = x + _L0_ffn_ref(_layernorm(x, axis=-1), L0_ffn_Wg, L0_ffn_W0a, L0_ffn_b0a, L0_ffn_W0b, L0_ffn_b0b, L0_ffn_W1a, L0_ffn_b1a, L0_ffn_W1b, L0_ffn_b1b)
    return x

_drawn_inputs = setup_inputs


def setup_inputs(seed=0):
    import zlib

    import numpy as np

    out = dict(_drawn_inputs(seed))
    spreads = {}
    factors = {'L0_ffn_b0a': 6.217, 'L0_ffn_b0b': 2.916, 'L0_ffn_b1a': 5.067, 'L0_ffn_b1b': 2.784}
    for name, (base, spread) in spreads.items():
        noise = np.random.default_rng([zlib.crc32(name.encode()), seed]).standard_normal(out[name].shape)
        drawn = base * np.exp(spread * noise) if base else spread * noise
        out[name] = jnp.asarray(drawn.astype(out[name].dtype))
    for name, factor in factors.items():
        out[name] = (out[name] * factor).astype(out[name].dtype)
    return out
```

```python
from contextlib import ExitStack

import concourse.bass as bass
from concourse import mybir

F32 = mybir.dt.float32
BF16 = mybir.dt.bfloat16
ACT = mybir.ActivationFunctionType
ALU = mybir.AluOpType
AX = mybir.AxisListType

B, C, L = 16, 128, 256
HEADS = 8
DH = C // HEADS
LC = L // 128
EXPERTS = 2
HID = 2 * L
HM = HID // 128
UNITS = EXPERTS * HM
PAIR = 2
TOK = PAIR * C
SLOTS = 4
EPS = 1e-5
SCALE = float(DH) ** -0.5
Q_PARTS = (0, 0, 0, 1, 1, 2)
K_PARTS = (0, 1, 2, 0, 1, 0)
STACK = DH * len(Q_PARTS)
ROWS = STACK + 2
STACK_INC = 16 * (len(Q_PARTS) + len(K_PARTS))
ORDER = (0, 2, 4, 6, 1, 3, 5, 7)
STEPS = B // PAIR
LOOPS = (STEPS - 2) // 2
LAST_C = 5
LD_INC = 4 * 16


def count(i, c, per=1, plus=0):
    return i * (SLOTS * per) + (c * per + plus)


def rounds(i, c, per):
    return i * per + (c // SLOTS + 1) * per


def build(nc, x, ctx, vt_pad, w1, w2, b1, b2, wg, gamma, out):
    with ExitStack() as stack:
        def sb(name, shape, dt=F32):
            return stack.enter_context(nc.sbuf_tensor(name, shape, dt))

        def pb(name, shape, dt=F32):
            return stack.enter_context(nc.psum_tensor(name, shape, dt))

        def sem(name):
            return stack.enter_context(nc.semaphore(name))

        xt = sb("xt", [128, SLOTS, L])
        qk = sb("qk", [128, SLOTS, 2, L])
        vt = sb("vt", [128, SLOTS, LC, HEADS, 32])
        w1t = sb("w1t", [128, LC, EXPERTS, HID])
        w2t = sb("w2t", [128, UNITS, L])
        b1t = sb("b1t", [128, UNITS])
        wgb = sb("wgb", [128, EXPERTS, L])
        gam = sb("gam", [128, 1])
        identf = sb("identf", [128, 128])
        identb = sb("identb", [128, 128], BF16)
        half = sb("half", [128, 2, 32])
        onesb = sb("onesb", [128, 128], BF16)
        power = sb("power", [128, 1])
        bias_f = sb("bias_f", [128, EXPERTS * L])
        bias_r = sb("bias_r", [128, EXPERTS * L])
        bias_p = sb("bias_p", [128, 3, EXPERTS * L], BF16)
        bias_rows = sb("bias_rows", [128, EXPERTS * L], BF16)
        mv1 = sb("mv1", [128, 2, 16])
        mv2 = sb("mv2", [128, 2, 16])
        rest = sb("rest", [128, 2, L])
        parts = sb("parts", [128, 2, 3, 2, L], BF16)
        qst = sb("qst", [128, SLOTS, HEADS, L], BF16)
        kst = sb("kst", [128, SLOTS, HEADS, L], BF16)
        nmax = sb("nmax", [128, 2, LC, HEADS])
        mparts = sb("mparts", [128, 2, LC, 2, HEADS], BF16)
        mrow = sb("mrow", [2 * HEADS, 2, L], BF16)
        P = sb("P", [128, 2, HEADS, LC, L])
        psum_l = sb("psum_l", [128, 2, HEADS, L])
        rden = sb("rden", [128, L])
        att = sb("att", [128, L])
        x1 = sb("x1", [128, SLOTS, L])
        xn = sb("xn", [128, 2, L])
        gate_prod = sb("gate_prod", [128, 2, L])
        logit = sb("logit", [128, SLOTS, EXPERTS])
        mask = sb("mask", [128, SLOTS, EXPERTS])
        xnT = sb("xnT", [128, 2, LC, TOK])
        hid = sb("hid", [128, 2, UNITS, TOK])
        yt = sb("yt", [128, 2, L])
        y = sb("y", [128, 2, L])

        smax = [pb(f"smax{n}", [128, LC, L]) for n in range(2)]
        st = [pb(f"st{n}", [128, LC, L]) for n in range(2)]
        od = pb("od", [128, 2, L])
        ff = [pb(f"ff{n}", [128, 2, TOK]) for n in range(2)]
        tr = pb("tr", [128, 512])
        tr_x = tr[:, 0:LC * 128].rearrange("p (a t) -> p a t", a=LC)
        tr_m = tr[0:2 * HEADS, 256:384].bitcast(BF16)

        s_ld = [sem(f"s_ld{n}") for n in range(SLOTS)]
        s_w = sem("s_w")
        s_small = sem("s_small")
        s_stk = [sem(f"s_stk{n}") for n in range(SLOTS)]
        s_mst = [sem(f"s_mst{n}") for n in range(SLOTS)]
        s_st = [sem(f"s_st{n}") for n in range(2)]
        s_const = sem("s_const")
        s_ones = sem("s_ones")
        s_bias = sem("s_bias")
        s_stat1, s_aggr1, s_var1, s_rstd1, s_qn = map(sem, ("s_stat1", "s_aggr1", "s_var1", "s_rstd1", "s_qn"))
        s_hi, s_rest, s_mid, s_rest2, s_lo = map(sem, ("s_hi", "s_rest", "s_mid", "s_rest2", "s_lo"))
        s_smax = sem("s_smax")
        s_max = sem("s_max")
        s_mhi, s_mmid = sem("s_mhi"), sem("s_mmid")
        s_mT = sem("s_mT")
        s_mrow = sem("s_mrow")
        s_sc = sem("s_sc")
        s_exp = sem("s_exp")
        s_add = sem("s_add")
        s_pv = sem("s_pv")
        s_rden, s_att, s_x1 = sem("s_rden"), sem("s_att"), sem("s_x1")
        s_stat2, s_aggr2, s_var2, s_rstd2, s_xn = map(sem, ("s_stat2", "s_aggr2", "s_var2", "s_rstd2", "s_xn"))
        s_logit = sem("s_logit")
        s_mask = sem("s_mask")
        s_xT, s_xTc = sem("s_xT"), sem("s_xTc")
        s_g1 = sem("s_g1")
        s_hid = sem("s_hid")
        s_g2 = sem("s_g2")
        s_y0, s_y = sem("s_y0"), sem("s_y")

        block = stack.enter_context(nc.Block())

        def steps(eng, step, tail):
            step(0, 0, first=True)
            with eng.Fori(0, LOOPS) as i:
                step(i, 2)
                step(i, 4)
            step(0, 2 * (STEPS - 1), last=True)
            tail()

        @block.sync
        def _(sp):
            def slot_free(i, c):
                if not (c < SLOTS and isinstance(i, int)):
                    sp.wait_ge(s_x1, count(i, c, 1, -3))

            def load(i, c):
                s = c % SLOTS
                b = count(i, c)
                sp.dma_start(xt[:, s, :], x[b]).then_inc(s_ld[s], 16)
                for n, src in enumerate((x, ctx)):
                    sp.dma_start(qk[:, s, n, :], src[b].rearrange("(h d) l -> d h l", d=DH)).then_inc(s_ld[s], 16)
                sp.dma_start(vt[:, s, :, :, :].rearrange("p a h d -> p (a h d)"), vt_pad[b]).then_inc(s_ld[s], 16)

            def stacks(i, c):
                s = c % SLOTS
                sp.wait_ge(s_lo, count(i, c, 1, 1))
                for r, (qp, kp) in enumerate(zip(Q_PARTS, K_PARTS)):
                    for dst, part, n in ((qst, qp, 0), (kst, kp, 1)):
                        sp.dma_start(dst[DH * r:DH * (r + 1), s, :, :],
                                     parts[:, c % 2, part, n, :]).then_inc(s_stk[s], 16)

            def max_rows(i, c):
                s = c % SLOTS
                sp.wait_ge(s_mrow, count(i, c, 1, 1))
                sp.dma_start(qst[STACK:ROWS, s, :, :], mrow[:, c % 2, :]).then_inc(s_mst[s], 16)

            def store(i, c):
                sp.wait_ge(s_y, count(i, c, 1, 1))
                sp.wait_ge(s_small, 64)
                sp.dma_start(out[count(i, c)], y[:, c % 2, :]).then_inc(s_st[c % 2], 16)

            def phase(i, c, last=False, ffn=True):
                n_left = B - c if last else SLOTS
                ends = c == LAST_C and not isinstance(i, int)
                if n_left > 3 and not ends:
                    slot_free(i, c + 3)
                    load(i, c + 3)
                if n_left > 2:
                    stacks(i, c + 2)
                if ends:
                    with sp.If(i < LOOPS - 1):
                        load(nc.s_assert_within(i, 0, LOOPS - 2), c + 3)
                if c % 2 and ffn:
                    store(i, c - 3)
                if n_left > 1:
                    max_rows(i, c + 1)
                if c % 2 and ffn:
                    store(i, c - 2)

            load(0, 0)
            sp.dma_start(bias_f[:, :], b2.partition_broadcast(128)).then_inc(s_small, 16)
            sp.dma_start(gam[:, :], gamma.partition_broadcast(128)).then_inc(s_small, 16)
            sp.dma_start(wgb[:, :, :].rearrange("p a c -> p (a c)"), wg.partition_broadcast(128)).then_inc(s_small, 16)
            sp.dma_start(b1t[:, :], b1).then_inc(s_small, 16)
            load(0, 1)
            load(0, 2)
            stacks(0, 0)
            stacks(0, 1)
            max_rows(0, 0)
            sp.dma_start(w1t[:, :, :, :].rearrange("p a e f -> p (a e f)"), w1).then_inc(s_w, 16)
            sp.dma_start(w2t[:, :, :].rearrange("p u l -> p (u l)"), w2).then_inc(s_w, 16)

            def step(i, c, first=False, last=False):
                phase(i, c, last, not first)
                phase(i, c + 1, last, not first)

            def tail():
                store(0, B - 2)
                store(0, B - 1)
                for n in range(2):
                    sp.wait_ge(s_st[n], 16 * (B // 2 + 1))

            steps(sp, step, tail)

        @block.gpsimd
        def _(pool):
            pool.memset(identf[:, :], 0.0).then_inc(s_const, 1)
            pool.memset(power[:, :], -0.5).then_inc(s_const, 1)
            pool.memset(half[:, :, :], 0.0).then_inc(s_const, 1)
            pool.wait_ge(s_const, 3)
            pool.affine_select(out=identf[:, :], in_=identf[:, :], compare_op=ALU.not_equal, fill=1.0,
                               base=0, pattern=[[-1, 128]], channel_multiplier=1).then_inc(s_const, 1)
            for e in range(2):
                pool.memset(half[:, e, 16 * e:16 * e + 16], 1.0).then_inc(s_const, 1)
            pool.wait_ge(s_const, 6)
            pool.tensor_copy(identb[:, :], identf[:, :]).then_inc(s_const, 1)

            def rstd(i, c, mv, s_var, s_rstd):
                pool.wait_ge(s_var, count(i, c, 1, 1))
                pool.tensor_tensor(mv[:, c % 2, 11:12], mv[:, c % 2, 10:11], power[:, :], ALU.pow).then_inc(s_rstd, 1)

            def rest1(i, c):
                if not (c < 1 and isinstance(i, int)):
                    pool.wait_ge(s_lo, count(i, c))
                pool.wait_ge(s_hi, count(i, c, 1, 1))
                pool.tensor_tensor(rest[:, :, :], qk[:, c % SLOTS, :, :], parts[:, c % 2, 0, :, :],
                                   ALU.subtract).then_inc(s_rest, 1)

            def rest2(i, c):
                pool.wait_ge(s_mid, count(i, c, 1, 1))
                pool.tensor_tensor(parts[:, c % 2, 2, :, :], rest[:, :, :], parts[:, c % 2, 1, :, :],
                                   ALU.subtract).then_inc(s_lo, 1)

            def add(i, c, k):
                h = ORDER[k]
                pool.wait_ge(s_exp, count(i, c, HEADS, k + 1))
                pool.tensor_tensor(psum_l[:, c % 2, h, :], P[:, c % 2, h, 0, :], P[:, c % 2, h, 1, :],
                                   ALU.add).then_inc(s_add, 1)

            for c in range(2):
                rstd(0, c, mv1, s_var1, s_rstd1)
                rest1(0, c)
                rest2(0, c)

            def phase(i, c, last=False):
                prep = not last or c + 2 < B
                if prep:
                    rstd(i, c + 2, mv1, s_var1, s_rstd1)
                if not (c < 2 and isinstance(i, int)):
                    pool.wait_ge(s_pv, count(i, c, 1, -1))
                for k in range(HEADS):
                    if k == 2 and not (c < 1 and isinstance(i, int)):
                        rstd(i, c - 1, mv2, s_var2, s_rstd2)
                    if k == 3 and prep:
                        rest1(i, c + 2)
                    if k == 5 and prep:
                        rest2(i, c + 2)
                    add(i, c, k)

            def step(i, c, first=False, last=False):
                phase(i, c, last)
                phase(i, c + 1, last)

            steps(pool, step, lambda: rstd(0, B - 1, mv2, s_var2, s_rstd2))

        @block.vector
        def _(dve):
            for n in range(2):
                dve.sem_inc(s_st[n], 16)
            dve.memset(kst[STACK:ROWS, :, :, :], 1.0).then_inc(s_ones, 1)
            dve.memset(onesb[:, :], 1.0).then_inc(s_ones, 1)
            dve.memset(bias_rows[:, :], 0.0).then_inc(s_ones, 1)

            def stats(i, c, src, mv, s_stat, s_aggr, s_var):
                m = mv[:, c % 2, :]
                dve.bn_stats(m[:, 0:6], src).then_inc(s_stat, 1)
                dve.wait_ge(s_stat, count(i, c, 1, 1))
                dve.memset(m[:, 12:13], 0.0)
                dve.bn_aggr(m[:, 8:10], m[:, 0:6]).then_inc(s_aggr, 1)
                dve.wait_ge(s_aggr, count(i, c, 1, 1))
                dve.tensor_scalar_add(m[:, 10:11], m[:, 9:10], EPS).then_inc(s_var, 1)

            def stats1(i, c):
                s = c % SLOTS
                dve.wait_ge(s_ld[s], rounds(i, c, LD_INC))
                stats(i, c, qk[:, s, 0, :], mv1, s_stat1, s_aggr1, s_var1)

            def normalise(i, c, dst, src, mv, s_rstd, s_done):
                m = mv[:, c % 2, :]
                dve.wait_ge(s_rstd, count(i, c, 1, 1))
                dve.tensor_scalar(dst, src, m[:, 8:9], m[:, 11:12], ALU.subtract, ALU.mult).then_inc(s_done, 1)

            def q_norm(i, c):
                s = c % SLOTS
                normalise(i, c, qk[:, s, 0, :], qk[:, s, 0, :], mv1, s_rstd1, s_qn)

            def take_max(i, c, k):
                dve.wait_ge(s_smax, count(i, c, HEADS, k + 1))
                dve.tensor_reduce(nmax[:, c % 2, :, ORDER[k]], smax[k % 2][:, :, :], AX.X, ALU.max,
                                  negate=True).then_inc(s_max, 1)

            def split_max(i, c):
                dve.wait_ge(s_max, count(i, c + 1, HEADS))
                dve.tensor_copy(mparts[:, c % 2, :, 0, :], nmax[:, c % 2, :, :]).then_inc(s_mhi, 1)
                dve.wait_ge(s_mhi, count(i, c, 1, 1))
                dve.tensor_tensor(mparts[:, c % 2, :, 1, :], nmax[:, c % 2, :, :], mparts[:, c % 2, :, 0, :],
                                  ALU.subtract).then_inc(s_mmid, 1)

            def post_recip(i, c):
                dve.wait_ge(s_pv, count(i, c, 1, 1))
                dve.reciprocal(rden[:, :], od[:, 1, :]).then_inc(s_rden, 1)

            def post_scale(i, c):
                dve.wait_ge(s_rden, count(i, c, 1, 1))
                dve.scalar_tensor_tensor(out=att[:, :], in0=od[:, 0, :], scalar=gam[:, 0:1], in1=rden[:, :],
                                         op0=ALU.mult, op1=ALU.mult).then_inc(s_att, 1)

            def post_add(i, c):
                dve.wait_ge(s_att, count(i, c, 1, 1))
                dve.tensor_tensor(x1[:, c % SLOTS, :], att[:, :], xt[:, c % SLOTS, :], ALU.add).then_inc(s_x1, 1)

            def stats2(i, c):
                dve.wait_ge(s_x1, count(i, c, 1, 1))
                stats(i, c, x1[:, c % SLOTS, :], mv2, s_stat2, s_aggr2, s_var2)

            def x_norm(i, c):
                normalise(i, c, xn[:, c % 2, :], x1[:, c % SLOTS, :], mv2, s_rstd2, s_xn)

            def gate(i, c):
                s = c % SLOTS
                dve.wait_ge(s_xn, count(i, c, 1, 1))
                if not (c < 1 and isinstance(i, int)):
                    dve.wait_ge(s_logit, count(i, c, 2))
                for e in range(EXPERTS):
                    dve.tensor_tensor_reduce(out=gate_prod[:, e, :], in0=xn[:, c % 2, :], in1=wgb[:, e, :],
                                             scale=1.0, scalar=0.0, op0=ALU.mult, op1=ALU.add,
                                             accum_out=logit[:, s, e:e + 1]).then_inc(s_logit, 1)
                dve.wait_ge(s_logit, count(i, c, 2, 2))
                for e, op in enumerate((ALU.is_ge, ALU.is_lt)):
                    dve.tensor_tensor(mask[:, s, e:e + 1], logit[:, s, 0:1], logit[:, s, 1:2], op).then_inc(s_mask, 1)

            def final(i, c):
                s, t = c % SLOTS, c % 2
                dve.wait_ge(s_g2, count(i, c, 1, 1))
                dve.wait_ge(s_mask, count(i, c, 2, 2))
                dve.scalar_tensor_tensor(out=yt[:, t, :], in0=ff[t][:, 0, :], scalar=mask[:, s, 0:1],
                                         in1=x1[:, s, :], op0=ALU.mult, op1=ALU.add).then_inc(s_y0, 1)
                dve.wait_ge(s_y0, count(i, c, 1, 1))
                dve.wait_ge(s_st[t], i * (SLOTS // 2 * 16) + (c // 2 + 1) * 16)
                dve.scalar_tensor_tensor(out=y[:, t, :], in0=ff[t][:, 1, :], scalar=mask[:, s, 1:2],
                                         in1=yt[:, t, :], op0=ALU.mult, op1=ALU.add).then_inc(s_y, 1)

            for c in range(2):
                stats1(0, c)
            for c in range(2):
                q_norm(0, c)
            dve.wait_ge(s_small, 64)
            dve.tensor_copy(bias_p[:, 0, :], bias_f[:, :]).then_inc(s_bias, 1)
            dve.wait_ge(s_bias, 1)
            dve.tensor_tensor(bias_r[:, :], bias_f[:, :], bias_p[:, 0, :], ALU.subtract).then_inc(s_bias, 1)
            dve.wait_ge(s_bias, 2)
            dve.tensor_copy(bias_p[:, 1, :], bias_r[:, :]).then_inc(s_bias, 1)
            dve.wait_ge(s_bias, 3)
            dve.tensor_tensor(bias_p[:, 2, :], bias_r[:, :], bias_p[:, 1, :], ALU.subtract).then_inc(s_bias, 1)
            dve.wait_ge(s_bias, 4)
            dve.wait_ge(s_ones, 3)
            for n in range(3):
                dve.tensor_copy(bias_rows[32 * n:32 * n + 1, :], bias_p[32 * n:32 * n + 1, n, :]).then_inc(s_bias, 1)
            for k in range(HEADS):
                take_max(0, 0, k)
            split_max(0, 0)

            def phase(i, c, last=False, ffn=True):
                n_left = B - c if last else SLOTS
                before = not (c < 1 and isinstance(i, int))
                if n_left > 2:
                    stats1(i, c + 2)
                if before:
                    post_recip(i, c - 1)
                for k in range(HEADS):
                    if n_left > 1:
                        take_max(i, c + 1, k)
                    if before and k == 0:
                        post_scale(i, c - 1)
                        post_add(i, c - 1)
                    if before and k == 1:
                        stats2(i, c - 1)
                    if n_left > 2 and k == 2:
                        q_norm(i, c + 2)
                    if before and k == 3:
                        x_norm(i, c - 1)
                    if before and k == 4:
                        gate(i, c - 1)
                    if ffn and c % 2 and k == 5:
                        final(i, c - 3)
                if n_left > 1:
                    split_max(i, c + 1)
                if ffn and c % 2:
                    final(i, c - 2)

            def step(i, c, first=False, last=False):
                phase(i, c, last, not first)
                phase(i, c + 1, last, not first)

            def tail():
                c = B - 1
                post_recip(0, c)
                post_scale(0, c)
                post_add(0, c)
                stats2(0, c)
                x_norm(0, c)
                gate(0, c)
                final(0, B - 2)
                final(0, B - 1)

            steps(dve, step, tail)

        @block.scalar
        def _(act):
            def copy_hi(i, c):
                s = c % SLOTS
                act.wait_ge(s_ld[s], rounds(i, c, LD_INC))
                act.wait_ge(s_qn, count(i, c, 1, 1))
                if not (c < 2 and isinstance(i, int)):
                    act.wait_ge(s_stk[s ^ 2], rounds(i, c - 2, STACK_INC))
                act.activation(parts[:, c % 2, 0, :, :], qk[:, s, :, :], ACT.Copy).then_inc(s_hi, 1)

            def copy_mid(i, c):
                act.wait_ge(s_rest, count(i, c, 1, 1))
                act.activation(parts[:, c % 2, 1, :, :], rest[:, :, :], ACT.Copy).then_inc(s_mid, 1)

            def exp(i, c, k):
                act.wait_ge(s_sc, count(i, c, HEADS, k + 1))
                act.activation(P[:, c % 2, ORDER[k], :, :], st[k % 2][:, :, :], ACT.Exp,
                               scale=SCALE).then_inc(s_exp, 1)

            def copy_max_rows(i, c):
                if not (c < 2 and isinstance(i, int)):
                    act.wait_ge(s_mst[(c - 2) % SLOTS], rounds(i, c - 2, 16))
                act.wait_ge(s_mT, count(i, c, 1, 1))
                act.activation(mrow[:, c % 2, :], tr_m, ACT.Copy).then_inc(s_mrow, 1)

            def copy_xT(i, c):
                t = c % 2
                act.wait_ge(s_xT, count(i, c, 1, 1))
                act.activation(xnT[:, c // 2 % 2, :, t * C:(t + 1) * C], tr_x, ACT.Copy).then_inc(s_xTc, 1)

            def hidden(i, c, u):
                if u % 2 == 0:
                    act.wait_ge(s_g1, count(i, c, UNITS // 4, u // 2 + 1))
                act.activation(hid[:, c // 2 % 2, u, :], ff[u // 2 % 2][:, u % 2, :],
                               ACT.Gelu if u < HM else ACT.Relu, bias=b1t[:, u:u + 1]).then_inc(s_hid, 1)

            for c in range(2):
                copy_hi(0, c)
                copy_mid(0, c)
            copy_max_rows(0, 0)
            act.wait_ge(s_small, 64)

            def phase(i, c, last=False, ffn=True):
                n_left = B - c if last else SLOTS
                before = not (c < 1 and isinstance(i, int))
                if not (c < 2 and isinstance(i, int)):
                    act.wait_ge(s_pv, count(i, c, 1, -1))
                for k in range(HEADS):
                    exp(i, c, k)
                    if k == 3 and n_left > 2:
                        copy_hi(i, c + 2)
                    if k == 4 and before:
                        copy_xT(i, c - 1)
                    if k == 5 and n_left > 2:
                        copy_mid(i, c + 2)
                    if k == 5 and ffn and c % 2 == 0:
                        for u in range(HM):
                            hidden(i, c - 2, u)
                if ffn and c % 2 == 0:
                    for u in range(HM, UNITS):
                        hidden(i, c - 2, u)
                if n_left > 1:
                    copy_max_rows(i, c + 1)

            def step(i, c, first=False, last=False):
                phase(i, c, last, not first)
                phase(i, c + 1, last, not first)

            def tail():
                copy_xT(0, B - 1)
                for u in range(UNITS):
                    hidden(0, B - 2, u)

            steps(act, step, tail)

        @block.tensor
        def _(pe):
            def scores_for_max(i, c, k):
                s, h = c % SLOTS, ORDER[k]
                if k == 0:
                    pe.wait_ge(s_stk[s], rounds(i, c, STACK_INC))
                if not (c < 1 and k < 2 and isinstance(i, int)):
                    pe.wait_ge(s_max, count(i, c, HEADS, k - 1))
                for a in range(LC):
                    mm = pe.matmul(smax[k % 2][:, a, :], qst[0:STACK, s, h, a * 128:(a + 1) * 128],
                                   kst[0:STACK, s, h, :], start=True, stop=True)
                mm.then_inc(s_smax, 1)

            def scores(i, c, k):
                s, h = c % SLOTS, ORDER[k]
                if k == 0:
                    pe.wait_ge(s_mst[s], rounds(i, c, 16))
                if not (c < 1 and k < 2 and isinstance(i, int)):
                    pe.wait_ge(s_exp, count(i, c, HEADS, k - 1))
                for a in range(LC):
                    mm = pe.matmul(st[k % 2][:, a, :], kst[0:ROWS, s, h, a * 128:(a + 1) * 128],
                                   qst[0:ROWS, s, h, :], start=True, stop=True)
                mm.then_inc(s_sc, 1)

            def values(i, c, g):
                s, heads = c % SLOTS, ORDER[4 * g:4 * g + 4]
                pe.wait_ge(s_exp, count(i, c, HEADS, 4 * g + 4))
                if g == 0:
                    pe.wait_ge(s_ld[s], rounds(i, c, LD_INC))
                    if not (c < 1 and isinstance(i, int)):
                        pe.wait_ge(s_att, count(i, c))
                for a in range(LC):
                    for j, h in enumerate(heads):
                        pe.matmul(od[32 * j:32 * j + 32, 0, :], vt[:, s, a, h, :], P[:, c % 2, h, a, :],
                                  start=g == 0 and a == 0, stop=False)
                pe.wait_ge(s_add, count(i, c, HEADS, 4 * g + 4))
                for j, h in enumerate(heads):
                    mm = pe.matmul(od[32 * j:32 * j + 32, 1, :], half[:, g, :], psum_l[:, c % 2, h, :],
                                   start=False, stop=g == 1)
                if g == 1:
                    mm.then_inc(s_pv, 1)

            def transpose_max(i, c):
                pe.wait_ge(s_mmid, count(i, c, 1, 1))
                if not (c < 1 and isinstance(i, int)):
                    pe.wait_ge(s_mrow, count(i, c))
                if not (c < 2 and isinstance(i, int)):
                    pe.wait_ge(s_xTc, count(i, c, 1, -1))
                for a in range(LC):
                    mm = pe.transpose(tr_m[:, a * 128:(a + 1) * 128],
                                      mparts[:, c % 2, a, :, :].rearrange("p m h -> p (m h)"), identb[:, :])
                mm.then_inc(s_mT, 1)

            def transpose_x(i, c):
                pe.wait_ge(s_xn, count(i, c, 1, 1))
                if not (c < 1 and isinstance(i, int)):
                    pe.wait_ge(s_xTc, count(i, c))
                for a in range(LC):
                    mm = pe.transpose(tr_x[:, a, :], xn[:, c % 2, a * 128:(a + 1) * 128], identf[:, :])
                mm.then_inc(s_xT, 1)

            def gemm1(i, c, u):
                e, m = divmod(u, HM)
                if u == 0:
                    pe.wait_ge(s_xTc, count(i, c, 1, 2))
                if u >= 4 and u % 2 == 0:
                    pe.wait_ge(s_hid, count(i, c, UNITS // 2, u - 2))
                for a in range(LC):
                    mm = pe.matmul(ff[u // 2 % 2][:, u % 2, :], w1t[:, a, e, m * 128:(m + 1) * 128],
                                   xnT[:, c // 2 % 2, a, :], start=a == 0, stop=a == LC - 1)
                if u % 2:
                    mm.then_inc(s_g1, 1)

            def gemm2(i, c, n):
                t = c % 2
                if n == 0:
                    pe.wait_ge(s_hid, count(i, c - t, UNITS // 2, UNITS))
                    pe.matmul(ff[t][:, :, :], onesb[:, :], bias_rows[:, :], start=True, stop=False)
                for u in (2 * n, 2 * n + 1):
                    mm = pe.matmul(ff[t][:, u // HM, :], hid[:, c // 2 % 2, u, t * C:(t + 1) * C],
                                   w2t[:, u, :], start=False, stop=u == UNITS - 1)
                if n == 3:
                    mm.then_inc(s_g2, 1)

            pe.wait_ge(s_const, 7)
            for k in range(HEADS):
                scores_for_max(0, 0, k)
            transpose_max(0, 0)
            pe.wait_ge(s_ones, 3)
            pe.wait_ge(s_bias, 7)
            pe.wait_ge(s_w, 32)

            def phase(i, c, last=False, ffn=True):
                n_left = B - c if last else SLOTS
                before = not (c < 1 and isinstance(i, int))
                for k in range(HEADS):
                    if n_left > 1:
                        scores_for_max(i, c + 1, k)
                    scores(i, c, k)
                    if k == 3 and before:
                        transpose_x(i, c - 1)
                    if k == 5:
                        values(i, c, 0)
                    if ffn:
                        if c % 2 == 0 and k >= 4:
                            gemm1(i, c - 2, 2 * k - 8)
                            gemm1(i, c - 2, 2 * k - 7)
                        if c % 2:
                            gemm2(i, c - 3 + k // 4, k % 4)
                values(i, c, 1)
                if n_left > 1:
                    transpose_max(i, c + 1)

            def step(i, c, first=False, last=False):
                phase(i, c, last, not first)
                phase(i, c + 1, last, not first)

            def tail():
                transpose_x(0, B - 1)
                for u in range(UNITS):
                    gemm1(0, B - 2, u)
                for n in range(8):
                    gemm2(0, B - 2 + n // 4, n % 4)

            steps(pe, step, tail)


def kernel(x, ctx_2048, L0_xattn_gamma, L0_ffn_Wg, L0_ffn_W0a, L0_ffn_b0a, L0_ffn_W0b, L0_ffn_b0b,
           L0_ffn_W1a, L0_ffn_b1a, L0_ffn_W1b, L0_ffn_b1b):
    import concourse.bacc as bacc
    import numpy as np
    from concourse.bass_utils import run_bass_kernel_spmd

    f = np.ascontiguousarray
    ctx = np.asarray(ctx_2048)
    v = ctx.reshape(B, HEADS // 2, 2, DH, LC, 128).transpose(0, 5, 4, 1, 2, 3)
    vt_pad = np.zeros((B, 128, LC, HEADS // 2, 2, 32), ctx.dtype)
    for e in range(2):
        vt_pad[:, :, :, :, e, 16 * e:16 * e + 16] = v[:, :, :, :, e]
    w1 = np.stack([np.asarray(L0_ffn_W0a), np.asarray(L0_ffn_W1a)])
    w1 = w1.reshape(EXPERTS, HID, LC, 128).transpose(3, 2, 0, 1)
    w2 = np.stack([np.asarray(L0_ffn_W0b), np.asarray(L0_ffn_W1b)])
    w2 = w2.reshape(EXPERTS, L, HM, 128).transpose(3, 0, 2, 1)
    b1 = np.stack([np.asarray(L0_ffn_b0a), np.asarray(L0_ffn_b1a)]).reshape(UNITS, 128).T
    b2 = np.stack([np.asarray(L0_ffn_b0b), np.asarray(L0_ffn_b1b)])
    arrays = {
        "x": f(x), "ctx": f(ctx), "vt_pad": f(vt_pad.reshape(B, 128, -1)),
        "w1": f(w1.reshape(128, -1)), "w2": f(w2.reshape(128, -1)), "b1": f(b1),
        "b2": f(b2.reshape(-1)), "wg": f(np.asarray(L0_ffn_Wg).reshape(-1)),
        "gamma": f(np.asarray(L0_xattn_gamma).reshape(1)),
    }
    nc = bacc.Bacc("TRN2", target_bir_lowering=False, num_devices=1)
    args = [nc.dram_tensor(f"in_{n}", a.shape, F32, kind="ExternalInput").ap() for n, a in arrays.items()]
    out = nc.dram_tensor("out", (B, C, L), F32, kind="ExternalOutput").ap()
    build(nc, *args, out)
    r = run_bass_kernel_spmd(nc, [{f"in_{n}": a for n, a in arrays.items()}], core_ids=[0])
    return r.results[0]["out"]
```

```python
from contextlib import ExitStack

import concourse.bass as bass
from concourse import mybir

F32 = mybir.dt.float32
BF16 = mybir.dt.bfloat16
ACT = mybir.ActivationFunctionType
ALU = mybir.AluOpType
AX = mybir.AxisListType

B, C, L = 16, 128, 256
HEADS = 8
DH = C // HEADS
LC = L // 128
EXPERTS = 2
HID = 2 * L
HM = HID // 128
UNITS = EXPERTS * HM
PAIR = 2
TOK = PAIR * C
SLOTS = 4
EPS = 1e-5
SCALE = float(DH) ** -0.5
Q_PARTS = (0, 0, 0, 1, 1, 2)
K_PARTS = (0, 1, 2, 0, 1, 0)
STACK = DH * len(Q_PARTS)
ROWS = STACK + 2
STACK_INC = 16 * len(Q_PARTS)
ORDER = (0, 2, 4, 6, 1, 3, 5, 7)
STEPS = B // PAIR
LOOPS = (STEPS - 2) // 2
LAST_C = 5
LD_INC = 4 * 16


def count(i, c, per=1, plus=0):
    return i * (SLOTS * per) + (c * per + plus)


def rounds(i, c, per):
    return i * per + (c // SLOTS + 1) * per


def build(nc, x, ctx, vt_pad, w1, w2, b1, b2, wg, gamma, out):
    with ExitStack() as stack:
        def sb(name, shape, dt=F32):
            return stack.enter_context(nc.sbuf_tensor(name, shape, dt))

        def pb(name, shape, dt=F32):
            return stack.enter_context(nc.psum_tensor(name, shape, dt))

        def sem(name):
            return stack.enter_context(nc.semaphore(name))

        xt = sb("xt", [128, SLOTS, L])
        qk = sb("qk", [128, SLOTS, 2, L])
        vt = sb("vt", [128, SLOTS, LC, HEADS, 32])
        w1t = sb("w1t", [128, LC, EXPERTS, HID])
        w2t = sb("w2t", [128, UNITS, L])
        b1t = sb("b1t", [128, UNITS])
        wgb = sb("wgb", [128, EXPERTS, L])
        gam = sb("gam", [128, 1])
        identf = sb("identf", [128, 128])
        identb = sb("identb", [128, 128], BF16)
        half = sb("half", [128, 2, 32])
        onesb = sb("onesb", [128, 128], BF16)
        power = sb("power", [128, 1])
        bias_f = sb("bias_f", [128, EXPERTS * L])
        bias_r = sb("bias_r", [128, EXPERTS * L])
        bias_p = sb("bias_p", [128, 3, EXPERTS * L], BF16)
        bias_rows = sb("bias_rows", [128, EXPERTS * L], BF16)
        mv1 = sb("mv1", [128, 2, 16])
        mv2 = sb("mv2", [128, 2, 16])
        rest = sb("rest", [128, 2, L])
        parts = sb("parts", [128, 2, 2, 3, L], BF16)
        qkst = sb("qkst", [128, SLOTS, HEADS, 2, L], BF16)
        nmax = sb("nmax", [128, 2, LC, HEADS])
        mparts = sb("mparts", [128, 2, LC, 2, HEADS], BF16)
        mrow = sb("mrow", [2 * HEADS, 2, L], BF16)
        P = sb("P", [128, 2, HEADS, LC, L])
        psum_l = sb("psum_l", [128, 2, HEADS, L])
        rden = sb("rden", [128, L])
        att = sb("att", [128, L])
        x1 = sb("x1", [128, SLOTS, L])
        xn = sb("xn", [128, 2, L])
        gate_prod = sb("gate_prod", [128, 2, L])
        logit = sb("logit", [128, SLOTS, EXPERTS])
        mask = sb("mask", [128, SLOTS, EXPERTS])
        xnT = sb("xnT", [128, 2, LC, TOK])
        hid = sb("hid", [128, 2, UNITS, TOK])
        yt = sb("yt", [128, 2, L])
        y = sb("y", [128, 2, L])

        smax = [pb(f"smax{n}", [128, LC, L]) for n in range(2)]
        st = [pb(f"st{n}", [128, LC, L]) for n in range(2)]
        od = pb("od", [128, 2, L])
        ff = [pb(f"ff{n}", [128, 2, TOK]) for n in range(2)]
        tr = pb("tr", [128, 512])
        tr_x = tr[:, 0:LC * 128].rearrange("p (a t) -> p a t", a=LC)
        tr_m = tr[0:2 * HEADS, 256:384].bitcast(BF16)

        s_ld = [sem(f"s_ld{n}") for n in range(SLOTS)]
        s_w = sem("s_w")
        s_small = sem("s_small")
        s_stk = [sem(f"s_stk{n}") for n in range(SLOTS)]
        s_mst = [sem(f"s_mst{n}") for n in range(SLOTS)]
        s_st = [sem(f"s_st{n}") for n in range(2)]
        s_const = sem("s_const")
        s_ones = sem("s_ones")
        s_bias = sem("s_bias")
        s_stat1, s_aggr1, s_var1, s_rstd1, s_qn = map(sem, ("s_stat1", "s_aggr1", "s_var1", "s_rstd1", "s_qn"))
        s_hi, s_rest, s_mid, s_rest2, s_lo = map(sem, ("s_hi", "s_rest", "s_mid", "s_rest2", "s_lo"))
        s_smax = sem("s_smax")
        s_max = sem("s_max")
        s_mhi, s_mmid = sem("s_mhi"), sem("s_mmid")
        s_mT = sem("s_mT")
        s_mrow = sem("s_mrow")
        s_sc = sem("s_sc")
        s_exp = sem("s_exp")
        s_add = sem("s_add")
        s_pv = sem("s_pv")
        s_rden, s_att, s_x1 = sem("s_rden"), sem("s_att"), sem("s_x1")
        s_stat2, s_aggr2, s_var2, s_rstd2, s_xn = map(sem, ("s_stat2", "s_aggr2", "s_var2", "s_rstd2", "s_xn"))
        s_logit = sem("s_logit")
        s_mask = sem("s_mask")
        s_xT, s_xTc = sem("s_xT"), sem("s_xTc")
        s_g1 = sem("s_g1")
        s_hid = sem("s_hid")
        s_g2 = sem("s_g2")
        s_y0, s_y = sem("s_y0"), sem("s_y")

        block = stack.enter_context(nc.Block())

        def steps(eng, step, tail):
            step(0, 0, first=True)
            with eng.Fori(0, LOOPS) as i:
                step(i, 2)
                step(i, 4)
            step(0, 2 * (STEPS - 1), last=True)
            tail()

        @block.sync
        def _(sp):
            def slot_free(i, c):
                if not (c < SLOTS and isinstance(i, int)):
                    sp.wait_ge(s_x1, count(i, c, 1, -3))

            def load(i, c):
                s = c % SLOTS
                b = count(i, c)
                sp.dma_start(xt[:, s, :], x[b]).then_inc(s_ld[s], 16)
                for n, src in enumerate((x, ctx)):
                    sp.dma_start(qk[:, s, n, :], src[b].rearrange("(h d) l -> d h l", d=DH)).then_inc(s_ld[s], 16)
                sp.dma_start(vt[:, s, :, :, :].rearrange("p a h d -> p (a h d)"), vt_pad[b]).then_inc(s_ld[s], 16)

            def stacks(i, c):
                s = c % SLOTS
                sp.wait_ge(s_lo, count(i, c, 1, 1))
                six = parts[:, c % 2, :, :, :].rearrange("p n a l -> p (n a) l")
                for r, (qp, kp) in enumerate(zip(Q_PARTS, K_PARTS)):
                    sp.dma_start(qkst[DH * r:DH * (r + 1), s, :, :, :],
                                 six[:, qp:kp + 4:kp + 3 - qp, :]).then_inc(s_stk[s], 16)

            def store(i, c):
                sp.wait_ge(s_y, count(i, c, 1, 1))
                sp.wait_ge(s_small, 64)
                sp.dma_start(out[count(i, c)], y[:, c % 2, :]).then_inc(s_st[c % 2], 16)

            def phase(i, c, last=False, ffn=True):
                n_left = B - c if last else SLOTS
                if c % 2 and ffn:
                    store(i, c - 3)
                if n_left > 3:
                    if c == LAST_C and not isinstance(i, int):
                        with sp.If(i < LOOPS - 1):
                            load(nc.s_assert_within(i, 0, LOOPS - 2), c + 3)
                    else:
                        slot_free(i, c + 3)
                        load(i, c + 3)
                if n_left > 2:
                    stacks(i, c + 2)
                if c % 2 and ffn:
                    store(i, c - 2)

            load(0, 0)
            sp.dma_start(bias_f[:, :], b2.partition_broadcast(128)).then_inc(s_small, 16)
            sp.dma_start(gam[:, :], gamma.partition_broadcast(128)).then_inc(s_small, 16)
            sp.dma_start(wgb[:, :, :].rearrange("p a c -> p (a c)"), wg.partition_broadcast(128)).then_inc(s_small, 16)
            sp.dma_start(b1t[:, :], b1).then_inc(s_small, 16)
            load(0, 1)
            load(0, 2)
            stacks(0, 0)
            stacks(0, 1)
            sp.dma_start(w1t[:, :, :, :].rearrange("p a e f -> p (a e f)"), w1).then_inc(s_w, 16)
            sp.dma_start(w2t[:, :, :].rearrange("p u l -> p (u l)"), w2).then_inc(s_w, 16)

            def step(i, c, first=False, last=False):
                phase(i, c, last, not first)
                phase(i, c + 1, last, not first)

            def tail():
                store(0, B - 2)
                store(0, B - 1)
                for n in range(2):
                    sp.wait_ge(s_st[n], 16 * (B // 2 + 1))

            steps(sp, step, tail)

        @block.gpsimd
        def _(pool):
            pool.memset(identf[:, :], 0.0).then_inc(s_const, 1)
            pool.memset(power[:, :], -0.5).then_inc(s_const, 1)
            pool.memset(half[:, :, :], 0.0).then_inc(s_const, 1)
            pool.wait_ge(s_const, 3)
            pool.affine_select(out=identf[:, :], in_=identf[:, :], compare_op=ALU.not_equal, fill=1.0,
                               base=0, pattern=[[-1, 128]], channel_multiplier=1).then_inc(s_const, 1)
            for e in range(2):
                pool.memset(half[:, e, 16 * e:16 * e + 16], 1.0).then_inc(s_const, 1)
            pool.wait_ge(s_const, 6)
            pool.tensor_copy(identb[:, :], identf[:, :]).then_inc(s_const, 1)

            def rstd(i, c, mv, s_var, s_rstd):
                pool.wait_ge(s_var, count(i, c, 1, 1))
                pool.tensor_tensor(mv[:, c % 2, 11:12], mv[:, c % 2, 10:11], power[:, :], ALU.pow).then_inc(s_rstd, 1)

            def rest1(i, c):
                if not (c < 1 and isinstance(i, int)):
                    pool.wait_ge(s_lo, count(i, c))
                pool.wait_ge(s_hi, count(i, c, 1, 1))
                pool.tensor_tensor(rest[:, :, :], qk[:, c % SLOTS, :, :], parts[:, c % 2, :, 0, :],
                                   ALU.subtract).then_inc(s_rest, 1)

            def rest2(i, c):
                pool.wait_ge(s_mid, count(i, c, 1, 1))
                pool.tensor_tensor(parts[:, c % 2, :, 2, :], rest[:, :, :], parts[:, c % 2, :, 1, :],
                                   ALU.subtract).then_inc(s_lo, 1)

            def add(i, c, k):
                h = ORDER[k]
                pool.wait_ge(s_exp, count(i, c, HEADS, k + 1))
                pool.tensor_tensor(psum_l[:, c % 2, h, :], P[:, c % 2, h, 0, :], P[:, c % 2, h, 1, :],
                                   ALU.add).then_inc(s_add, 1)

            for c in range(2):
                rstd(0, c, mv1, s_var1, s_rstd1)
                rest1(0, c)
                rest2(0, c)

            def phase(i, c, last=False):
                prep = not last or c + 2 < B
                if not (c < 2 and isinstance(i, int)):
                    pool.wait_ge(s_pv, count(i, c, 1, -1))
                for k in range(HEADS):
                    add(i, c, k)
                    if k == 0 and prep:
                        rstd(i, c + 2, mv1, s_var1, s_rstd1)
                    if k == 1 and not (c < 1 and isinstance(i, int)):
                        rstd(i, c - 1, mv2, s_var2, s_rstd2)
                    if k == 2 and prep:
                        rest1(i, c + 2)
                    if k == 4 and prep:
                        rest2(i, c + 2)

            def step(i, c, first=False, last=False):
                phase(i, c, last)
                phase(i, c + 1, last)

            steps(pool, step, lambda: rstd(0, B - 1, mv2, s_var2, s_rstd2))

        @block.vector
        def _(dve):
            for n in range(2):
                dve.sem_inc(s_st[n], 16)
            dve.memset(qkst[STACK:ROWS, :, :, 1, :], 1.0).then_inc(s_ones, 1)
            dve.memset(onesb[:, :], 1.0).then_inc(s_ones, 1)
            dve.memset(bias_rows[:, :], 0.0).then_inc(s_ones, 1)

            def stats(i, c, src, mv, s_stat):
                dve.bn_stats(mv[:, c % 2, 0:6], src).then_inc(s_stat, 1)

            def aggregate(i, c, mv, s_stat, s_aggr):
                dve.wait_ge(s_stat, count(i, c, 1, 1))
                dve.memset(mv[:, c % 2, 12:13], 0.0)
                dve.bn_aggr(mv[:, c % 2, 8:10], mv[:, c % 2, 0:6]).then_inc(s_aggr, 1)

            def add_eps(i, c, mv, s_aggr, s_var):
                dve.wait_ge(s_aggr, count(i, c, 1, 1))
                dve.tensor_scalar_add(mv[:, c % 2, 10:11], mv[:, c % 2, 9:10], EPS).then_inc(s_var, 1)

            def stats1(i, c):
                s = c % SLOTS
                dve.wait_ge(s_ld[s], rounds(i, c, LD_INC))
                stats(i, c, qk[:, s, 0, :], mv1, s_stat1)

            def normalise(i, c, dst, src, mv, s_rstd, s_done):
                m = mv[:, c % 2, :]
                dve.wait_ge(s_rstd, count(i, c, 1, 1))
                dve.tensor_scalar(dst, src, m[:, 8:9], m[:, 11:12], ALU.subtract, ALU.mult).then_inc(s_done, 1)

            def q_norm(i, c):
                s = c % SLOTS
                normalise(i, c, qk[:, s, 0, :], qk[:, s, 0, :], mv1, s_rstd1, s_qn)

            def take_max(i, c, k):
                dve.wait_ge(s_smax, count(i, c, HEADS, k + 1))
                dve.tensor_reduce(nmax[:, c % 2, :, ORDER[k]], smax[k % 2][:, :, :], AX.X, ALU.max,
                                  negate=True).then_inc(s_max, 1)

            def split_max(i, c):
                dve.wait_ge(s_max, count(i, c + 1, HEADS))
                dve.tensor_copy(mparts[:, c % 2, :, 0, :], nmax[:, c % 2, :, :]).then_inc(s_mhi, 1)
                dve.wait_ge(s_mhi, count(i, c, 1, 1))
                dve.tensor_tensor(mparts[:, c % 2, :, 1, :], nmax[:, c % 2, :, :], mparts[:, c % 2, :, 0, :],
                                  ALU.subtract).then_inc(s_mmid, 1)

            def post_recip(i, c):
                dve.wait_ge(s_pv, count(i, c, 1, 1))
                dve.reciprocal(rden[:, :], od[:, 1, :]).then_inc(s_rden, 1)

            def post_scale(i, c):
                dve.wait_ge(s_rden, count(i, c, 1, 1))
                dve.scalar_tensor_tensor(out=att[:, :], in0=od[:, 0, :], scalar=gam[:, 0:1], in1=rden[:, :],
                                         op0=ALU.mult, op1=ALU.mult).then_inc(s_att, 1)

            def post_add(i, c):
                dve.wait_ge(s_att, count(i, c, 1, 1))
                dve.tensor_tensor(x1[:, c % SLOTS, :], att[:, :], xt[:, c % SLOTS, :], ALU.add).then_inc(s_x1, 1)

            def stats2(i, c):
                dve.wait_ge(s_x1, count(i, c, 1, 1))
                stats(i, c, x1[:, c % SLOTS, :], mv2, s_stat2)

            def x_norm(i, c):
                normalise(i, c, xn[:, c % 2, :], x1[:, c % SLOTS, :], mv2, s_rstd2, s_xn)

            def gate(i, c):
                s = c % SLOTS
                dve.wait_ge(s_xn, count(i, c, 1, 1))
                if not (c < 1 and isinstance(i, int)):
                    dve.wait_ge(s_logit, count(i, c, 2))
                for e in range(EXPERTS):
                    dve.tensor_tensor_reduce(out=gate_prod[:, e, :], in0=xn[:, c % 2, :], in1=wgb[:, e, :],
                                             scale=1.0, scalar=0.0, op0=ALU.mult, op1=ALU.add,
                                             accum_out=logit[:, s, e:e + 1]).then_inc(s_logit, 1)
                dve.wait_ge(s_logit, count(i, c, 2, 2))
                for e, op in enumerate((ALU.is_ge, ALU.is_lt)):
                    dve.tensor_tensor(mask[:, s, e:e + 1], logit[:, s, 0:1], logit[:, s, 1:2], op).then_inc(s_mask, 1)

            def final(i, c):
                s, t = c % SLOTS, c % 2
                dve.wait_ge(s_g2, count(i, c, 1, 1))
                dve.wait_ge(s_mask, count(i, c, 2, 2))
                dve.scalar_tensor_tensor(out=yt[:, t, :], in0=ff[t][:, 0, :], scalar=mask[:, s, 0:1],
                                         in1=x1[:, s, :], op0=ALU.mult, op1=ALU.add).then_inc(s_y0, 1)
                dve.wait_ge(s_y0, count(i, c, 1, 1))
                dve.wait_ge(s_st[t], i * (SLOTS // 2 * 16) + (c // 2 + 1) * 16)
                dve.scalar_tensor_tensor(out=y[:, t, :], in0=ff[t][:, 1, :], scalar=mask[:, s, 1:2],
                                         in1=yt[:, t, :], op0=ALU.mult, op1=ALU.add).then_inc(s_y, 1)

            for c in range(2):
                stats1(0, c)
                aggregate(0, c, mv1, s_stat1, s_aggr1)
                add_eps(0, c, mv1, s_aggr1, s_var1)
            for c in range(2):
                q_norm(0, c)
            dve.wait_ge(s_small, 64)
            dve.tensor_copy(bias_p[:, 0, :], bias_f[:, :]).then_inc(s_bias, 1)
            dve.wait_ge(s_bias, 1)
            dve.tensor_tensor(bias_r[:, :], bias_f[:, :], bias_p[:, 0, :], ALU.subtract).then_inc(s_bias, 1)
            dve.wait_ge(s_bias, 2)
            dve.tensor_copy(bias_p[:, 1, :], bias_r[:, :]).then_inc(s_bias, 1)
            dve.wait_ge(s_bias, 3)
            dve.tensor_tensor(bias_p[:, 2, :], bias_r[:, :], bias_p[:, 1, :], ALU.subtract).then_inc(s_bias, 1)
            dve.wait_ge(s_bias, 4)
            dve.wait_ge(s_ones, 3)
            for n in range(3):
                dve.tensor_copy(bias_rows[32 * n:32 * n + 1, :], bias_p[32 * n:32 * n + 1, n, :]).then_inc(s_bias, 1)
            for k in range(HEADS):
                take_max(0, 0, k)
            split_max(0, 0)

            def phase(i, c, last=False, ffn=True):
                n_left = B - c if last else SLOTS
                before = not (c < 1 and isinstance(i, int))
                prep = n_left > 2
                if prep:
                    stats1(i, c + 2)
                if before:
                    post_recip(i, c - 1)
                if prep:
                    aggregate(i, c + 2, mv1, s_stat1, s_aggr1)
                if before:
                    post_scale(i, c - 1)
                if prep:
                    add_eps(i, c + 2, mv1, s_aggr1, s_var1)
                if before:
                    post_add(i, c - 1)
                    stats2(i, c - 1)
                    aggregate(i, c - 1, mv2, s_stat2, s_aggr2)
                    add_eps(i, c - 1, mv2, s_aggr2, s_var2)
                if prep:
                    q_norm(i, c + 2)
                for k in range(HEADS):
                    if n_left > 1:
                        take_max(i, c + 1, k)
                    if k == c % 2 and before:
                        x_norm(i, c - 1)
                    if before and k == 3:
                        gate(i, c - 1)
                    if ffn and c % 2 and k == 5:
                        final(i, c - 3)
                if n_left > 1:
                    split_max(i, c + 1)
                if ffn and c % 2:
                    final(i, c - 2)

            def step(i, c, first=False, last=False):
                phase(i, c, last, not first)
                phase(i, c + 1, last, not first)

            def tail():
                c = B - 1
                post_recip(0, c)
                post_scale(0, c)
                post_add(0, c)
                stats2(0, c)
                aggregate(0, c, mv2, s_stat2, s_aggr2)
                add_eps(0, c, mv2, s_aggr2, s_var2)
                x_norm(0, c)
                gate(0, c)
                final(0, B - 2)
                final(0, B - 1)

            steps(dve, step, tail)

        @block.scalar
        def _(act):
            def copy_hi(i, c):
                s = c % SLOTS
                act.wait_ge(s_ld[s], rounds(i, c, LD_INC))
                act.wait_ge(s_qn, count(i, c, 1, 1))
                if not (c < 2 and isinstance(i, int)):
                    act.wait_ge(s_stk[s ^ 2], rounds(i, c - 2, STACK_INC))
                act.activation(parts[:, c % 2, :, 0, :], qk[:, s, :, :], ACT.Copy).then_inc(s_hi, 1)

            def copy_mid(i, c):
                act.wait_ge(s_rest, count(i, c, 1, 1))
                act.activation(parts[:, c % 2, :, 1, :], rest[:, :, :], ACT.Copy).then_inc(s_mid, 1)

            def exp(i, c, k):
                act.wait_ge(s_sc, count(i, c, HEADS, k + 1))
                act.activation(P[:, c % 2, ORDER[k], :, :], st[k % 2][:, :, :], ACT.Exp,
                               scale=SCALE).then_inc(s_exp, 1)

            def copy_max_rows(i, c):
                if not (c < 2 and isinstance(i, int)):
                    act.wait_ge(s_mst[(c - 2) % SLOTS], rounds(i, c - 2, 16))
                act.wait_ge(s_mT, count(i, c, 1, 1))
                act.activation(mrow[:, c % 2, :], tr_m, ACT.Copy).then_inc(s_mrow, 1)
                act.wait_ge(s_mrow, count(i, c, 1, 1))
                act.dma_start(qkst[STACK:ROWS, c % SLOTS, :, 0, :], mrow[:, c % 2, :]).then_inc(s_mst[c % SLOTS], 16)

            def copy_xT(i, c):
                t = c % 2
                act.wait_ge(s_xT, count(i, c, 1, 1))
                act.activation(xnT[:, c // 2 % 2, :, t * C:(t + 1) * C], tr_x, ACT.Copy).then_inc(s_xTc, 1)

            def hidden(i, c, u):
                if u % 2 == 0:
                    act.wait_ge(s_g1, count(i, c, UNITS // 4, u // 2 + 1))
                act.activation(hid[:, c // 2 % 2, u, :], ff[u // 2 % 2][:, u % 2, :],
                               ACT.Gelu if u < HM else ACT.Relu, bias=b1t[:, u:u + 1]).then_inc(s_hid, 1)

            for c in range(2):
                copy_hi(0, c)
                copy_mid(0, c)
            copy_max_rows(0, 0)
            act.wait_ge(s_small, 64)

            def phase(i, c, last=False, ffn=True):
                n_left = B - c if last else SLOTS
                before = not (c < 1 and isinstance(i, int))
                if not (c < 2 and isinstance(i, int)):
                    act.wait_ge(s_pv, count(i, c, 1, -1))
                for k in range(HEADS):
                    exp(i, c, k)
                    if k == 2 and n_left > 2:
                        copy_hi(i, c + 2)
                    if k == 4 and before:
                        copy_xT(i, c - 1)
                    if k == 4 and n_left > 2:
                        copy_mid(i, c + 2)
                    if k == 6 and n_left > 1 and c % 2:
                        copy_max_rows(i, c + 1)
                for u in range(UNITS):
                    if ffn and c % 2 == 0:
                        hidden(i, c - 2, u)
                    if u == 5 and n_left > 1 and c % 2 == 0:
                        copy_max_rows(i, c + 1)

            def step(i, c, first=False, last=False):
                phase(i, c, last, not first)
                phase(i, c + 1, last, not first)

            def tail():
                copy_xT(0, B - 1)
                for u in range(UNITS):
                    hidden(0, B - 2, u)

            steps(act, step, tail)

        @block.tensor
        def _(pe):
            def scores_for_max(i, c, k):
                s, h = c % SLOTS, ORDER[k]
                if k == 0:
                    pe.wait_ge(s_stk[s], rounds(i, c, STACK_INC))
                if not (c < 1 and k < 2 and isinstance(i, int)):
                    pe.wait_ge(s_max, count(i, c, HEADS, k - 1))
                for a in range(LC):
                    mm = pe.matmul(smax[k % 2][:, a, :], qkst[0:STACK, s, h, 0, a * 128:(a + 1) * 128],
                                   qkst[0:STACK, s, h, 1, :], start=True, stop=True)
                mm.then_inc(s_smax, 1)

            def scores(i, c, k):
                s, h = c % SLOTS, ORDER[k]
                if k == 0:
                    pe.wait_ge(s_mst[s], rounds(i, c, 16))
                if not (c < 1 and k < 2 and isinstance(i, int)):
                    pe.wait_ge(s_exp, count(i, c, HEADS, k - 1))
                for a in range(LC):
                    mm = pe.matmul(st[k % 2][:, a, :], qkst[0:ROWS, s, h, 1, a * 128:(a + 1) * 128],
                                   qkst[0:ROWS, s, h, 0, :], start=True, stop=True)
                mm.then_inc(s_sc, 1)

            def values(i, c, g):
                s, heads = c % SLOTS, ORDER[4 * g:4 * g + 4]
                pe.wait_ge(s_exp, count(i, c, HEADS, 4 * g + 4))
                if g == 0:
                    pe.wait_ge(s_ld[s], rounds(i, c, LD_INC))
                    if not (c < 1 and isinstance(i, int)):
                        pe.wait_ge(s_att, count(i, c))
                for a in range(LC):
                    for j, h in enumerate(heads):
                        pe.matmul(od[32 * j:32 * j + 32, 0, :], vt[:, s, a, h, :], P[:, c % 2, h, a, :],
                                  start=g == 0 and a == 0, stop=False)

            def sums(i, c, g):
                pe.wait_ge(s_add, count(i, c, HEADS, 4 * g + 4))
                for j, h in enumerate(ORDER[4 * g:4 * g + 4]):
                    mm = pe.matmul(od[32 * j:32 * j + 32, 1, :], half[:, g, :], psum_l[:, c % 2, h, :],
                                   start=False, stop=g == 1)
                if g == 1:
                    mm.then_inc(s_pv, 1)

            def transpose_max(i, c):
                pe.wait_ge(s_mmid, count(i, c, 1, 1))
                if not (c < 1 and isinstance(i, int)):
                    pe.wait_ge(s_mrow, count(i, c))
                if not (c < 2 and isinstance(i, int)):
                    pe.wait_ge(s_xTc, count(i, c, 1, -1))
                for a in range(LC):
                    mm = pe.transpose(tr_m[:, a * 128:(a + 1) * 128],
                                      mparts[:, c % 2, a, :, :].rearrange("p m h -> p (m h)"), identb[:, :])
                mm.then_inc(s_mT, 1)

            def transpose_x(i, c):
                pe.wait_ge(s_xn, count(i, c, 1, 1))
                if not (c < 1 and isinstance(i, int)):
                    pe.wait_ge(s_xTc, count(i, c))
                for a in range(LC):
                    mm = pe.transpose(tr_x[:, a, :], xn[:, c % 2, a * 128:(a + 1) * 128], identf[:, :])
                mm.then_inc(s_xT, 1)

            def gemm1(i, c, u):
                e, m = divmod(u, HM)
                if u == 0:
                    pe.wait_ge(s_xTc, count(i, c, 1, 2))
                if u >= 4 and u % 2 == 0:
                    pe.wait_ge(s_hid, count(i, c, UNITS // 2, u - 2))
                for a in range(LC):
                    mm = pe.matmul(ff[u // 2 % 2][:, u % 2, :], w1t[:, a, e, m * 128:(m + 1) * 128],
                                   xnT[:, c // 2 % 2, a, :], start=a == 0, stop=a == LC - 1)
                if u % 2:
                    mm.then_inc(s_g1, 1)

            def gemm2(i, c, n):
                t = c % 2
                pe.wait_ge(s_hid, count(i, c - t, UNITS // 2, UNITS if t or n == 3 else UNITS - 2))
                if n == 0:
                    pe.matmul(ff[t][:, :, :], onesb[:, :], bias_rows[:, :], start=True, stop=False)
                for u in (2 * n, 2 * n + 1):
                    mm = pe.matmul(ff[t][:, u // HM, :], hid[:, c // 2 % 2, u, t * C:(t + 1) * C],
                                   w2t[:, u, :], start=False, stop=u == UNITS - 1)
                if n == 3:
                    mm.then_inc(s_g2, 1)

            pe.wait_ge(s_const, 7)
            for k in range(HEADS):
                scores_for_max(0, 0, k)
            transpose_max(0, 0)
            pe.wait_ge(s_ones, 3)
            pe.wait_ge(s_bias, 7)
            pe.wait_ge(s_w, 32)

            def phase(i, c, last=False, ffn=True):
                n_left = B - c if last else SLOTS
                before = not (c < 1 and isinstance(i, int))
                after, even = n_left > 1, c % 2 == 0
                for k in range(HEADS):
                    if k >= 6:
                        scores(i, c, k)
                    if ffn and not even:
                        gemm2(i, c - 3 + k // 4, k % 4)
                    if k < 6:
                        scores(i, c, k)
                    if after and even and k >= 3:
                        scores_for_max(i, c + 1, k - 3)
                    if after and not even and 1 <= k <= 4:
                        scores_for_max(i, c + 1, 2 * k - 2)
                        scores_for_max(i, c + 1, 2 * k - 1)
                    if k == (4 if even else 3) and before:
                        transpose_x(i, c - 1)
                    if k == 5:
                        values(i, c, 0)
                        if after and not even:
                            transpose_max(i, c + 1)
                    if k == 6:
                        sums(i, c, 0)
                    if ffn and even and k >= 5:
                        gemm1(i, c - 2, k - 5)
                if even:
                    if after:
                        scores_for_max(i, c + 1, 5)
                    if ffn:
                        gemm1(i, c - 2, 3)
                    values(i, c, 1)
                    for k in (6, 7):
                        if after:
                            scores_for_max(i, c + 1, k)
                        if ffn:
                            gemm1(i, c - 2, k - 2)
                    sums(i, c, 1)
                    if after:
                        transpose_max(i, c + 1)
                    if ffn:
                        gemm1(i, c - 2, 6)
                        gemm1(i, c - 2, 7)
                else:
                    values(i, c, 1)
                    sums(i, c, 1)

            def step(i, c, first=False, last=False):
                phase(i, c, last, not first)
                phase(i, c + 1, last, not first)

            def tail():
                transpose_x(0, B - 1)
                for u in range(UNITS):
                    gemm1(0, B - 2, u)
                for n in range(8):
                    gemm2(0, B - 2 + n // 4, n % 4)

            steps(pe, step, tail)


def kernel(x, ctx_2048, L0_xattn_gamma, L0_ffn_Wg, L0_ffn_W0a, L0_ffn_b0a, L0_ffn_W0b, L0_ffn_b0b,
           L0_ffn_W1a, L0_ffn_b1a, L0_ffn_W1b, L0_ffn_b1b):
    import concourse.bacc as bacc
    import numpy as np
    from concourse.bass_utils import run_bass_kernel_spmd

    f = np.ascontiguousarray
    ctx = np.asarray(ctx_2048)
    v = ctx.reshape(B, HEADS // 2, 2, DH, LC, 128).transpose(0, 5, 4, 1, 2, 3)
    vt_pad = np.zeros((B, 128, LC, HEADS // 2, 2, 32), ctx.dtype)
    for e in range(2):
        vt_pad[:, :, :, :, e, 16 * e:16 * e + 16] = v[:, :, :, :, e]
    w1 = np.stack([np.asarray(L0_ffn_W0a), np.asarray(L0_ffn_W1a)])
    w1 = w1.reshape(EXPERTS, HID, LC, 128).transpose(3, 2, 0, 1)
    w2 = np.stack([np.asarray(L0_ffn_W0b), np.asarray(L0_ffn_W1b)])
    w2 = w2.reshape(EXPERTS, L, HM, 128).transpose(3, 0, 2, 1)
    b1 = np.stack([np.asarray(L0_ffn_b0a), np.asarray(L0_ffn_b1a)]).reshape(UNITS, 128).T
    b2 = np.stack([np.asarray(L0_ffn_b0b), np.asarray(L0_ffn_b1b)])
    arrays = {
        "x": f(x), "ctx": f(ctx), "vt_pad": f(vt_pad.reshape(B, 128, -1)),
        "w1": f(w1.reshape(128, -1)), "w2": f(w2.reshape(128, -1)), "b1": f(b1),
        "b2": f(b2.reshape(-1)), "wg": f(np.asarray(L0_ffn_Wg).reshape(-1)),
        "gamma": f(np.asarray(L0_xattn_gamma).reshape(1)),
    }
    nc = bacc.Bacc("TRN2", target_bir_lowering=False, num_devices=1)
    args = [nc.dram_tensor(f"in_{n}", a.shape, F32, kind="ExternalInput").ap() for n, a in arrays.items()]
    out = nc.dram_tensor("out", (B, C, L), F32, kind="ExternalOutput").ap()
    build(nc, *args, out)
    r = run_bass_kernel_spmd(nc, [{f"in_{n}": a for n, a in arrays.items()}], core_ids=[0])
    return r.results[0]["out"]
```

```python
from contextlib import ExitStack

import concourse.bass as bass
from concourse import mybir

F32 = mybir.dt.float32
BF16 = mybir.dt.bfloat16
ACT = mybir.ActivationFunctionType
ALU = mybir.AluOpType
AX = mybir.AxisListType

B, C, L = 16, 128, 256
HEADS = 8
DH = C // HEADS
LC = L // 128
EXPERTS = 2
HID = 2 * L
HM = HID // 128
UNITS = EXPERTS * HM
PAIR = 2
TOK = PAIR * C
SLOTS = 4
EPS = 1e-5
SCALE = float(DH) ** -0.5
Q_PARTS = (0, 0, 0, 1, 1, 2)
K_PARTS = (0, 1, 2, 0, 1, 0)
STACK = DH * len(Q_PARTS)
ROWS = STACK + 2
STACK_INC = 16 * len(Q_PARTS)
ORDER = (0, 2, 4, 6, 1, 3, 5, 7)
STEPS = B // PAIR
LOOPS = (STEPS - 2) // 2
LAST_C = 5
LD_INC = 4 * 16


def count(i, c, per=1, plus=0):
    return i * (SLOTS * per) + (c * per + plus)


def rounds(i, c, per):
    return i * per + (c // SLOTS + 1) * per


def at_least(i, c, n):
    return c >= n


def prepares(i, c):
    return not isinstance(i, int) or 0 < c < B - 2


def has_next(i, c):
    return not isinstance(i, int) or c + 1 < B


def build(nc, x, ctx, vt_pad, w1, w2, b1, b2, wg, gamma, out):
    with ExitStack() as stack:
        def sb(name, shape, dt=F32):
            return stack.enter_context(nc.sbuf_tensor(name, shape, dt))

        def pb(name, shape, dt=F32):
            return stack.enter_context(nc.psum_tensor(name, shape, dt))

        def sem(name):
            return stack.enter_context(nc.semaphore(name))

        xt = sb("xt", [128, SLOTS, L])
        qk = sb("qk", [128, SLOTS, 2, L])
        vt = sb("vt", [128, SLOTS, LC, HEADS, 32])
        w1t = sb("w1t", [128, LC, EXPERTS, HID])
        w2t = sb("w2t", [128, UNITS, L])
        b1t = sb("b1t", [128, UNITS])
        wgb = sb("wgb", [128, EXPERTS, L])
        gam = sb("gam", [128, 1])
        identf = sb("identf", [128, 128])
        identb = sb("identb", [128, 128], BF16)
        half = sb("half", [128, 2, 32])
        onesb = sb("onesb", [128, 128], BF16)
        power = sb("power", [128, 1])
        bias_f = sb("bias_f", [128, EXPERTS * L])
        bias_r = sb("bias_r", [128, EXPERTS * L])
        bias_p = sb("bias_p", [128, 3, EXPERTS * L], BF16)
        bias_rows = sb("bias_rows", [128, EXPERTS * L], BF16)
        mv1 = sb("mv1", [128, 2, 16])
        mv2 = sb("mv2", [128, 2, 16])
        rest = sb("rest", [128, 2, L])
        parts = sb("parts", [128, 2, 2, 3, L], BF16)
        qkst = sb("qkst", [128, SLOTS, HEADS, 2, L], BF16)
        nmax = sb("nmax", [128, 2, LC, HEADS])
        mparts = sb("mparts", [128, 2, LC, 2, HEADS], BF16)
        mrow = sb("mrow", [2 * HEADS, 2, L], BF16)
        P = sb("P", [128, 2, HEADS, LC, L])
        psum_l = sb("psum_l", [128, 2, HEADS, L])
        rden = sb("rden", [128, L])
        att = sb("att", [128, L])
        x1 = sb("x1", [128, SLOTS, L])
        xn = sb("xn", [128, 2, L])
        gate_prod = sb("gate_prod", [128, 2, L])
        logit = sb("logit", [128, SLOTS, EXPERTS])
        mask = sb("mask", [128, SLOTS, EXPERTS])
        xnT = sb("xnT", [128, 2, LC, TOK])
        hid = sb("hid", [128, 2, UNITS, TOK])
        yt = sb("yt", [128, 2, L])
        y = sb("y", [128, 2, L])

        smax = [pb(f"smax{n}", [128, LC, L]) for n in range(2)]
        st = [pb(f"st{n}", [128, LC, L]) for n in range(2)]
        od = pb("od", [128, 2, L])
        ff = [pb(f"ff{n}", [128, 2, TOK]) for n in range(2)]
        tr = pb("tr", [128, 512])
        tr_x = tr[:, 0:LC * 128].rearrange("p (a t) -> p a t", a=LC)
        tr_m = tr[0:2 * HEADS, 256:384].bitcast(BF16)

        s_ld = [sem(f"s_ld{n}") for n in range(SLOTS)]
        s_w = sem("s_w")
        s_small = sem("s_small")
        s_stk = [sem(f"s_stk{n}") for n in range(SLOTS)]
        s_mst = [sem(f"s_mst{n}") for n in range(SLOTS)]
        s_st = [sem(f"s_st{n}") for n in range(2)]
        s_const = sem("s_const")
        s_ones = sem("s_ones")
        s_kones = sem("s_kones")
        s_bias = sem("s_bias")
        s_stat1, s_aggr1, s_var1, s_rstd1, s_qn = map(sem, ("s_stat1", "s_aggr1", "s_var1", "s_rstd1", "s_qn"))
        s_hi, s_rest, s_mid, s_rest2, s_lo = map(sem, ("s_hi", "s_rest", "s_mid", "s_rest2", "s_lo"))
        s_smax = sem("s_smax")
        s_max = sem("s_max")
        s_mhi, s_mmid = sem("s_mhi"), sem("s_mmid")
        s_mT = sem("s_mT")
        s_mrow = sem("s_mrow")
        s_sc = sem("s_sc")
        s_exp = sem("s_exp")
        s_add = sem("s_add")
        s_pv = sem("s_pv")
        s_rden, s_att, s_x1 = sem("s_rden"), sem("s_att"), sem("s_x1")
        s_stat2, s_aggr2, s_var2, s_rstd2, s_xn = map(sem, ("s_stat2", "s_aggr2", "s_var2", "s_rstd2", "s_xn"))
        s_logit = sem("s_logit")
        s_mask = sem("s_mask")
        s_xT, s_xTc = sem("s_xT"), sem("s_xTc")
        s_g1 = sem("s_g1")
        s_hid = sem("s_hid")
        s_g2 = sem("s_g2")
        s_y0, s_y = sem("s_y0"), sem("s_y")

        block = stack.enter_context(nc.Block())

        def steps(eng, step, tail):
            step(0, 0, first=True)
            with eng.Fori(0, LOOPS) as i:
                step(i, 2)
                step(i, 4)
            step(0, 2 * (STEPS - 1), last=True)
            tail()

        def half_steps(eng, start, rest, tail):
            rest(0, 0, ffn=False)
            start(0, 1)
            rest(0, 1, ffn=False)
            start(0, 2)
            with eng.Fori(0, LOOPS) as i:
                for c in (2, 3, 4, 5):
                    rest(i, c)
                    start(i, c + 1)
            rest(0, 14)
            start(0, 15)
            rest(0, 15)
            tail()

        @block.sync
        def _(sp):
            def slot_free(i, c):
                if not (c < SLOTS and isinstance(i, int)):
                    sp.wait_ge(s_x1, count(i, c, 1, -3))

            def load(i, c):
                s = c % SLOTS
                b = count(i, c)
                sp.dma_start(xt[:, s, :], x[b]).then_inc(s_ld[s], 16)
                for n, src in enumerate((x, ctx)):
                    sp.dma_start(qk[:, s, n, :], src[b].rearrange("(h d) l -> d h l", d=DH)).then_inc(s_ld[s], 16)
                sp.dma_start(vt[:, s, :, :, :].rearrange("p a h d -> p (a h d)"), vt_pad[b]).then_inc(s_ld[s], 16)

            def stacks(i, c, early=False):
                s = c % SLOTS
                six = parts[:, c % 2, :, :, :].rearrange("p n a l -> p (n a) l")
                order = list(enumerate(zip(Q_PARTS, K_PARTS)))
                if early:
                    order.sort(key=lambda entry: max(entry[1]))
                else:
                    sp.wait_ge(s_lo, count(i, c, 1, 1))
                for r, (qp, kp) in order:
                    if early:
                        sp.wait_ge((s_hi, s_mid, s_lo)[max(qp, kp)], count(i, c, 1, 1))
                    sp.dma_start(qkst[DH * r:DH * (r + 1), s, :, :, :],
                                 six[:, qp:kp + 4:kp + 3 - qp, :]).then_inc(s_stk[s], 16)

            def max_rows(i, c):
                sp.wait_ge(s_mrow, count(i, c, 1, 1))
                sp.dma_start(qkst[STACK:ROWS, c % SLOTS, :, 0, :], mrow[:, c % 2, :]).then_inc(s_mst[c % SLOTS], 16)

            def store(i, c):
                sp.wait_ge(s_y, count(i, c, 1, 1))
                sp.wait_ge(s_small, 64)
                sp.dma_start(out[count(i, c)], y[:, c % 2, :]).then_inc(s_st[c % 2], 16)

            def phase(i, c, last=False, ffn=True):
                n_left = B - c if last else SLOTS
                ends = c == LAST_C and not isinstance(i, int)
                if n_left > 3:
                    if ends:
                        sp.wait_ge(s_small, 64)
                    slot_free(i, c + 3)
                    if ends:
                        with sp.If(i < LOOPS - 1):
                            load(nc.s_assert_within(i, 0, LOOPS - 2), c + 3)
                    else:
                        load(i, c + 3)
                if n_left > 1 and c % 2 == 0:
                    max_rows(i, c + 1)
                if prepares(i, c):
                    stacks(i, c + 2)
                if n_left > 1 and c % 2:
                    max_rows(i, c + 1)
                if c % 2 and ffn:
                    store(i, c - 3)
                    store(i, c - 2)

            load(0, 0)
            load(0, 1)
            load(0, 2)
            sp.dma_start(bias_f[:, :], b2.partition_broadcast(128)).then_inc(s_small, 16)
            sp.dma_start(gam[:, :], gamma.partition_broadcast(128)).then_inc(s_small, 16)
            sp.dma_start(wgb[:, :, :].rearrange("p a c -> p (a c)"), wg.partition_broadcast(128)).then_inc(s_small, 16)
            sp.dma_start(b1t[:, :], b1).then_inc(s_small, 16)
            for c in range(3):
                stacks(0, c, early=True)
            max_rows(0, 0)
            sp.dma_start(w1t[:, :, :, :].rearrange("p a e f -> p (a e f)"), w1).then_inc(s_w, 16)
            sp.dma_start(w2t[:, :, :].rearrange("p u l -> p (u l)"), w2).then_inc(s_w, 16)

            def step(i, c, first=False, last=False):
                phase(i, c, last, not first)
                phase(i, c + 1, last, not first)

            def tail():
                store(0, B - 2)
                store(0, B - 1)
                for n in range(2):
                    sp.wait_ge(s_st[n], 16 * (B // 2 + 1))

            steps(sp, step, tail)

        @block.gpsimd
        def _(pool):
            pool.memset(identf[:, :], 0.0).then_inc(s_const, 1)
            pool.memset(power[:, :], -0.5).then_inc(s_const, 1)
            pool.memset(half[:, :, :], 0.0).then_inc(s_const, 1)
            pool.wait_ge(s_const, 3)
            pool.affine_select(out=identf[:, :], in_=identf[:, :], compare_op=ALU.not_equal, fill=1.0,
                               base=0, pattern=[[-1, 128]], channel_multiplier=1).then_inc(s_const, 1)
            for e in range(2):
                pool.memset(half[:, e, 16 * e:16 * e + 16], 1.0).then_inc(s_const, 1)
            pool.wait_ge(s_const, 6)
            pool.tensor_copy(identb[:, :], identf[:, :]).then_inc(s_const, 1)

            def row_of_ones(n):
                pool.wait_ge(s_const, 7)
                if n > 1:
                    pool.wait_ge(s_lo, 3)
                pool.memset(qkst[STACK:ROWS, n, :, 1, :], 1.0).then_inc(s_kones, 1)
                pool.wait_ge(s_kones, n + 1)

            for n in (0, 1):
                row_of_ones(n)

            def rstd(i, c, mv, s_var, s_rstd):
                pool.wait_ge(s_var, count(i, c, 1, 1))
                pool.tensor_tensor(mv[:, c % 2, 11:12], mv[:, c % 2, 10:11], power[:, :], ALU.pow).then_inc(s_rstd, 1)

            def rest1(i, c):
                if not (c < 1 and isinstance(i, int)):
                    pool.wait_ge(s_lo, count(i, c))
                pool.wait_ge(s_hi, count(i, c, 1, 1))
                pool.tensor_tensor(rest[:, :, :], qk[:, c % SLOTS, :, :], parts[:, c % 2, :, 0, :],
                                   ALU.subtract).then_inc(s_rest, 1)

            def rest2(i, c):
                pool.wait_ge(s_mid, count(i, c, 1, 1))
                pool.tensor_tensor(parts[:, c % 2, :, 2, :], rest[:, :, :], parts[:, c % 2, :, 1, :],
                                   ALU.subtract).then_inc(s_lo, 1)

            def add(i, c, k):
                h = ORDER[k]
                pool.wait_ge(s_exp, count(i, c, HEADS, k + 1))
                pool.tensor_tensor(psum_l[:, c % 2, h, :], P[:, c % 2, h, 0, :], P[:, c % 2, h, 1, :],
                                   ALU.add).then_inc(s_add, 1)

            for c in range(2):
                rstd(0, c, mv1, s_var1, s_rstd1)
            rest1(0, 1)
            rstd(0, 2, mv1, s_var1, s_rstd1)
            rest2(0, 1)
            rest1(0, 2)
            rest2(0, 2)
            for n in (2, 3):
                row_of_ones(n)

            def phase(i, c, last=False):
                prep = prepares(i, c)
                if not (c < 2 and isinstance(i, int)):
                    pool.wait_ge(s_pv, count(i, c, 1, -1))
                even = c % 2 == 0
                for k in range(HEADS):
                    add(i, c, k)
                    if even and k == 2 and c:
                        rstd(i, c - 1, mv2, s_var2, s_rstd2)
                    if k == 0 and prep:
                        rstd(i, c + 2, mv1, s_var1, s_rstd1)
                    if k == 2 and not even:
                        rstd(i, c - 1, mv2, s_var2, s_rstd2)
                    if k == (5 if even else 2) and prep:
                        rest1(i, c + 2)
                    if k == (7 if even else 3) and prep:
                        rest2(i, c + 2)

            def step(i, c, first=False, last=False):
                phase(i, c, last)
                phase(i, c + 1, last)

            steps(pool, step, lambda: rstd(0, B - 1, mv2, s_var2, s_rstd2))

        @block.vector
        def _(dve):
            for n in range(2):
                dve.sem_inc(s_st[n], 16)
            dve.memset(onesb[:, :], 1.0).then_inc(s_ones, 1)
            dve.memset(bias_rows[:, :], 0.0).then_inc(s_ones, 1)

            def stats(i, c, src, mv, s_stat):
                dve.bn_stats(mv[:, c % 2, 0:6], src).then_inc(s_stat, 1)

            def aggregate(i, c, mv, s_stat, s_aggr):
                dve.wait_ge(s_stat, count(i, c, 1, 1))
                dve.memset(mv[:, c % 2, 12:13], 0.0)
                dve.bn_aggr(mv[:, c % 2, 8:10], mv[:, c % 2, 0:6]).then_inc(s_aggr, 1)

            def add_eps(i, c, mv, s_aggr, s_var):
                dve.wait_ge(s_aggr, count(i, c, 1, 1))
                dve.tensor_scalar_add(mv[:, c % 2, 10:11], mv[:, c % 2, 9:10], EPS).then_inc(s_var, 1)

            def stats1(i, c):
                s = c % SLOTS
                dve.wait_ge(s_ld[s], rounds(i, c, LD_INC))
                stats(i, c, qk[:, s, 0, :], mv1, s_stat1)

            def normalise(i, c, dst, src, mv, s_rstd, s_done):
                m = mv[:, c % 2, :]
                dve.wait_ge(s_rstd, count(i, c, 1, 1))
                dve.tensor_scalar(dst, src, m[:, 8:9], m[:, 11:12], ALU.subtract, ALU.mult).then_inc(s_done, 1)

            def moments1(i, c):
                stats1(i, c)
                aggregate(i, c, mv1, s_stat1, s_aggr1)
                add_eps(i, c, mv1, s_aggr1, s_var1)

            def q_norm(i, c):
                s = c % SLOTS
                normalise(i, c, qk[:, s, 0, :], qk[:, s, 0, :], mv1, s_rstd1, s_qn)

            def take_max(i, c, k):
                dve.wait_ge(s_smax, count(i, c, HEADS, k + 1))
                dve.tensor_reduce(nmax[:, c % 2, :, ORDER[k]], smax[k % 2][:, :, :], AX.X, ALU.max,
                                  negate=True).then_inc(s_max, 1)

            def split_max(i, c):
                dve.wait_ge(s_max, count(i, c + 1, HEADS))
                dve.tensor_copy(mparts[:, c % 2, :, 0, :], nmax[:, c % 2, :, :]).then_inc(s_mhi, 1)
                dve.wait_ge(s_mhi, count(i, c, 1, 1))
                dve.tensor_tensor(mparts[:, c % 2, :, 1, :], nmax[:, c % 2, :, :], mparts[:, c % 2, :, 0, :],
                                  ALU.subtract).then_inc(s_mmid, 1)

            def post_recip(i, c):
                dve.wait_ge(s_pv, count(i, c, 1, 1))
                dve.reciprocal(rden[:, :], od[:, 1, :]).then_inc(s_rden, 1)

            def post_scale(i, c):
                dve.wait_ge(s_rden, count(i, c, 1, 1))
                dve.scalar_tensor_tensor(out=att[:, :], in0=od[:, 0, :], scalar=gam[:, 0:1], in1=rden[:, :],
                                         op0=ALU.mult, op1=ALU.mult).then_inc(s_att, 1)

            def post_add(i, c):
                dve.wait_ge(s_att, count(i, c, 1, 1))
                dve.tensor_tensor(x1[:, c % SLOTS, :], att[:, :], xt[:, c % SLOTS, :], ALU.add).then_inc(s_x1, 1)

            def stats2(i, c):
                dve.wait_ge(s_x1, count(i, c, 1, 1))
                stats(i, c, x1[:, c % SLOTS, :], mv2, s_stat2)

            def x_norm(i, c):
                normalise(i, c, xn[:, c % 2, :], x1[:, c % SLOTS, :], mv2, s_rstd2, s_xn)

            def gate(i, c):
                s = c % SLOTS
                dve.wait_ge(s_xn, count(i, c, 1, 1))
                if not (c < 1 and isinstance(i, int)):
                    dve.wait_ge(s_logit, count(i, c, 2))
                for e in range(EXPERTS):
                    dve.tensor_tensor_reduce(out=gate_prod[:, e, :], in0=xn[:, c % 2, :], in1=wgb[:, e, :],
                                             scale=1.0, scalar=0.0, op0=ALU.mult, op1=ALU.add,
                                             accum_out=logit[:, s, e:e + 1]).then_inc(s_logit, 1)
                dve.wait_ge(s_logit, count(i, c, 2, 2))
                for e, op in enumerate((ALU.is_ge, ALU.is_lt)):
                    dve.tensor_tensor(mask[:, s, e:e + 1], logit[:, s, 0:1], logit[:, s, 1:2], op).then_inc(s_mask, 1)

            def final_0(i, c):
                s, t = c % SLOTS, c % 2
                dve.wait_ge(s_g2, count(i, c, 1, 1))
                dve.wait_ge(s_mask, count(i, c, 2, 2))
                dve.scalar_tensor_tensor(out=yt[:, t, :], in0=ff[t][:, 0, :], scalar=mask[:, s, 0:1],
                                         in1=x1[:, s, :], op0=ALU.mult, op1=ALU.add).then_inc(s_y0, 1)

            def final_1(i, c):
                s, t = c % SLOTS, c % 2
                dve.wait_ge(s_y0, count(i, c, 1, 1))
                dve.wait_ge(s_st[t], i * (SLOTS // 2 * 16) + (c // 2 + 1) * 16)
                dve.scalar_tensor_tensor(out=y[:, t, :], in0=ff[t][:, 1, :], scalar=mask[:, s, 1:2],
                                         in1=yt[:, t, :], op0=ALU.mult, op1=ALU.add).then_inc(s_y, 1)

            def final(i, c):
                final_0(i, c)
                final_1(i, c)

            for c in range(2):
                moments1(0, c)
            q_norm(0, 0)
            dve.wait_ge(s_qn, 1)
            dve.tensor_copy(parts[:, 0, :, 0, :], qk[:, 0, :, :]).then_inc(s_hi, 1)
            q_norm(0, 1)
            dve.wait_ge(s_hi, 1)
            dve.tensor_tensor(rest[:, :, :], qk[:, 0, :, :], parts[:, 0, :, 0, :], ALU.subtract).then_inc(s_rest, 1)
            dve.wait_ge(s_rest, 1)
            dve.tensor_copy(parts[:, 0, :, 1, :], rest[:, :, :]).then_inc(s_mid, 1)
            dve.wait_ge(s_mid, 1)
            dve.tensor_tensor(parts[:, 0, :, 2, :], rest[:, :, :], parts[:, 0, :, 1, :], ALU.subtract).then_inc(s_lo, 1)
            moments1(0, 2)
            q_norm(0, 2)
            for k in range(HEADS):
                take_max(0, 0, k)
            split_max(0, 0)
            dve.wait_ge(s_small, 64)
            dve.tensor_copy(bias_p[:, 0, :], bias_f[:, :]).then_inc(s_bias, 1)
            dve.wait_ge(s_bias, 1)
            dve.tensor_tensor(bias_r[:, :], bias_f[:, :], bias_p[:, 0, :], ALU.subtract).then_inc(s_bias, 1)
            dve.wait_ge(s_bias, 2)
            dve.tensor_copy(bias_p[:, 1, :], bias_r[:, :]).then_inc(s_bias, 1)
            dve.wait_ge(s_bias, 3)
            dve.tensor_tensor(bias_p[:, 2, :], bias_r[:, :], bias_p[:, 1, :], ALU.subtract).then_inc(s_bias, 1)
            dve.wait_ge(s_bias, 4)
            dve.wait_ge(s_ones, 2)
            for n in range(3):
                dve.tensor_copy(bias_rows[32 * n:32 * n + 1, :], bias_p[32 * n:32 * n + 1, n, :]).then_inc(s_bias, 1)
            for k in range(4):
                take_max(0, 1, k)

            def start(i, c):
                if c % 2 == 0:
                    post_recip(i, c - 1)
                    if c < B:
                        take_max(i, c + 1, 0)
                    post_scale(i, c - 1)
                    if c < B:
                        take_max(i, c + 1, 1)
                    post_add(i, c - 1)
                    if c < B:
                        take_max(i, c + 1, 2)
                    stats2(i, c - 1)
                    aggregate(i, c - 1, mv2, s_stat2, s_aggr2)
                    add_eps(i, c - 1, mv2, s_aggr2, s_var2)
                    if c >= 4:
                        final_0(i, c - 3)
                    if c < B:
                        take_max(i, c + 1, 3)
                    if c >= 4:
                        final_1(i, c - 3)

            def rest_of(i, c, ffn=True):
                def maxima(*heads):
                    if has_next(i, c):
                        for k in heads:
                            take_max(i, c + 1, k)
                prep = prepares(i, c)
                if c % 2:
                    post_recip(i, c - 1)
                    if prep:
                        stats1(i, c + 2)
                    post_scale(i, c - 1)
                    if prep:
                        aggregate(i, c + 2, mv1, s_stat1, s_aggr1)
                    post_add(i, c - 1)
                    if prep:
                        add_eps(i, c + 2, mv1, s_aggr1, s_var1)
                    maxima(0)
                    stats2(i, c - 1)
                    maxima(1)
                    aggregate(i, c - 1, mv2, s_stat2, s_aggr2)
                    if prep:
                        q_norm(i, c + 2)
                    add_eps(i, c - 1, mv2, s_aggr2, s_var2)
                    maxima(2, 3)
                    x_norm(i, c - 1)
                    maxima(4, 5, 6, 7)
                else:
                    if c:
                        x_norm(i, c - 1)
                    if prep:
                        q_norm(i, c + 2)
                    maxima(4, 5, 6, 7)
                if has_next(i, c):
                    split_max(i, c + 1)
                if c % 2:
                    if isinstance(i, int):
                        if c + 3 < B:
                            moments1(i, c + 3)
                    elif c < LAST_C:
                        moments1(i, c + 3)
                    else:
                        with dve.If(i < LOOPS - 1):
                            moments1(nc.s_assert_within(i, 0, LOOPS - 2), c + 3)
                if c:
                    gate(i, c - 1)
                if ffn and c % 2:
                    final(i, c - 3)

            def tail():
                start(0, B)
                x_norm(0, B - 1)
                gate(0, B - 1)
                final(0, B - 2)
                final(0, B - 1)

            half_steps(dve, start, rest_of, tail)

        @block.scalar
        def _(act):
            def copy_hi(i, c):
                s = c % SLOTS
                act.wait_ge(s_ld[s], rounds(i, c, LD_INC))
                act.wait_ge(s_qn, count(i, c, 1, 1))
                if not (c < 2 and isinstance(i, int)):
                    act.wait_ge(s_stk[s ^ 2], rounds(i, c - 2, STACK_INC))
                act.activation(parts[:, c % 2, :, 0, :], qk[:, s, :, :], ACT.Copy).then_inc(s_hi, 1)

            def copy_mid(i, c):
                act.wait_ge(s_rest, count(i, c, 1, 1))
                act.activation(parts[:, c % 2, :, 1, :], rest[:, :, :], ACT.Copy).then_inc(s_mid, 1)

            def exp(i, c, k):
                act.wait_ge(s_sc, count(i, c, HEADS, k + 1))
                act.activation(P[:, c % 2, ORDER[k], :, :], st[k % 2][:, :, :], ACT.Exp,
                               scale=SCALE).then_inc(s_exp, 1)

            def copy_max_rows(i, c):
                if not (c < 2 and isinstance(i, int)):
                    act.wait_ge(s_mst[(c - 2) % SLOTS], rounds(i, c - 2, 16))
                act.wait_ge(s_mT, count(i, c, 1, 1))
                act.activation(mrow[:, c % 2, :], tr_m, ACT.Copy).then_inc(s_mrow, 1)

            def copy_xT(i, c):
                t = c % 2
                act.wait_ge(s_xT, count(i, c, 1, 1))
                act.activation(xnT[:, c // 2 % 2, :, t * C:(t + 1) * C], tr_x, ACT.Copy).then_inc(s_xTc, 1)

            def hidden(i, c, u):
                if u % 2 == 0:
                    act.wait_ge(s_g1, count(i, c, UNITS // 4, u // 2 + 1))
                act.activation(hid[:, c // 2 % 2, u, :], ff[u // 2 % 2][:, u % 2, :],
                               ACT.Gelu if u < HM else ACT.Relu, bias=b1t[:, u:u + 1]).then_inc(s_hid, 1)

            act.wait_ge(s_hi, 1)
            copy_hi(0, 1)
            copy_mid(0, 1)
            copy_hi(0, 2)
            copy_mid(0, 2)
            copy_max_rows(0, 0)
            act.wait_ge(s_small, 64)

            def phase(i, c, last=False, ffn=True):
                n_left = B - c if last else SLOTS
                before = not (c < 1 and isinstance(i, int))
                if not (c < 2 and isinstance(i, int)):
                    act.wait_ge(s_pv, count(i, c, 1, -1))
                for k in range(HEADS):
                    exp(i, c, k)
                    if k == (5 if c % 2 == 0 else 2) and prepares(i, c):
                        copy_hi(i, c + 2)
                    if k == (6 if c % 2 == 0 else 4) and before:
                        copy_xT(i, c - 1)
                    if k == (7 if c % 2 == 0 else 3) and prepares(i, c):
                        copy_mid(i, c + 2)
                    if k == 6 and n_left > 1 and c % 2:
                        copy_max_rows(i, c + 1)
                    if ffn and c % 2 and k in (1, 3):
                        hidden(i, c - 3, k + 3)
                        hidden(i, c - 3, k + 4)
                if c % 2 == 0:
                    if n_left > 1:
                        copy_max_rows(i, c + 1)
                    for u in range(HM):
                        if ffn:
                            hidden(i, c - 2, u)

            def step(i, c, first=False, last=False):
                phase(i, c, last, not first)
                phase(i, c + 1, last, not first)

            def tail():
                copy_xT(0, B - 1)
                for u in range(UNITS):
                    hidden(0, B - 2, u)

            steps(act, step, tail)

        @block.tensor
        def _(pe):
            def scores_for_max(i, c, k):
                s, h = c % SLOTS, ORDER[k]
                if k == 0:
                    pe.wait_ge(s_stk[s], rounds(i, c, STACK_INC))
                if not (c < 1 and k < 2 and isinstance(i, int)):
                    pe.wait_ge(s_max, count(i, c, HEADS, k - 1))
                for a in range(LC):
                    mm = pe.matmul(smax[k % 2][:, a, :], qkst[0:STACK, s, h, 0, a * 128:(a + 1) * 128],
                                   qkst[0:STACK, s, h, 1, :], start=True, stop=True)
                mm.then_inc(s_smax, 1)

            def scores(i, c, k):
                s, h = c % SLOTS, ORDER[k]
                if k == 0:
                    pe.wait_ge(s_mst[s], rounds(i, c, 16))
                if not (c < 1 and k < 2 and isinstance(i, int)):
                    pe.wait_ge(s_exp, count(i, c, HEADS, k - 1))
                for a in range(LC):
                    mm = pe.matmul(st[k % 2][:, a, :], qkst[0:ROWS, s, h, 1, a * 128:(a + 1) * 128],
                                   qkst[0:ROWS, s, h, 0, :], start=True, stop=True)
                mm.then_inc(s_sc, 1)

            def values(i, c, g):
                s, heads = c % SLOTS, ORDER[4 * g:4 * g + 4]
                pe.wait_ge(s_exp, count(i, c, HEADS, 4 * g + 4))
                if g == 0:
                    pe.wait_ge(s_ld[s], rounds(i, c, LD_INC))
                    if not (c < 1 and isinstance(i, int)):
                        pe.wait_ge(s_att, count(i, c))
                for a in range(LC):
                    for j, h in enumerate(heads):
                        pe.matmul(od[32 * j:32 * j + 32, 0, :], vt[:, s, a, h, :], P[:, c % 2, h, a, :],
                                  start=g == 0 and a == 0, stop=False)

            def sums(i, c, g):
                pe.wait_ge(s_add, count(i, c, HEADS, 4 * g + 4))
                for j, h in enumerate(ORDER[4 * g:4 * g + 4]):
                    mm = pe.matmul(od[32 * j:32 * j + 32, 1, :], half[:, g, :], psum_l[:, c % 2, h, :],
                                   start=False, stop=g == 1)
                if g == 1:
                    mm.then_inc(s_pv, 1)

            def transpose_max(i, c):
                pe.wait_ge(s_mmid, count(i, c, 1, 1))
                if not (c < 1 and isinstance(i, int)):
                    pe.wait_ge(s_mrow, count(i, c))
                if not (c < 2 and isinstance(i, int)):
                    pe.wait_ge(s_xTc, count(i, c, 1, -1))
                for a in range(LC):
                    mm = pe.transpose(tr_m[:, a * 128:(a + 1) * 128],
                                      mparts[:, c % 2, a, :, :].rearrange("p m h -> p (m h)"), identb[:, :])
                mm.then_inc(s_mT, 1)

            def transpose_x(i, c):
                pe.wait_ge(s_xn, count(i, c, 1, 1))
                if not (c < 1 and isinstance(i, int)):
                    pe.wait_ge(s_xTc, count(i, c))
                for a in range(LC):
                    mm = pe.transpose(tr_x[:, a, :], xn[:, c % 2, a * 128:(a + 1) * 128], identf[:, :])
                mm.then_inc(s_xT, 1)

            def gemm1(i, c, u):
                e, m = divmod(u, HM)
                if u == 0:
                    pe.wait_ge(s_xTc, count(i, c, 1, 2))
                if u >= 4 and u % 2 == 0:
                    pe.wait_ge(s_hid, count(i, c, UNITS // 2, u - 2))
                for a in range(LC):
                    mm = pe.matmul(ff[u // 2 % 2][:, u % 2, :], w1t[:, a, e, m * 128:(m + 1) * 128],
                                   xnT[:, c // 2 % 2, a, :], start=a == 0, stop=a == LC - 1)
                if u % 2:
                    mm.then_inc(s_g1, 1)

            def gemm2(i, c, n):
                t = c % 2
                pe.wait_ge(s_hid, count(i, c - t, UNITS // 2, UNITS if t or n == 3 else UNITS - 2))
                if n == 0:
                    pe.matmul(ff[t][:, :, :], onesb[:, :], bias_rows[:, :], start=True, stop=False)
                for u in (2 * n, 2 * n + 1):
                    mm = pe.matmul(ff[t][:, u // HM, :], hid[:, c // 2 % 2, u, t * C:(t + 1) * C],
                                   w2t[:, u, :], start=False, stop=u == UNITS - 1)
                if n == 3:
                    mm.then_inc(s_g2, 1)

            pe.wait_ge(s_const, 7)
            for k in range(HEADS):
                scores_for_max(0, 0, k)
            transpose_max(0, 0)
            pe.wait_ge(s_kones, 1)
            for k in range(4):
                scores(0, 0, k)
                scores_for_max(0, 1, k)

            def start(i, c):
                if c % 2 == 0:
                    for k in range(4):
                        if c >= 4:
                            gemm2(i, c - 3, k)
                        if c < B:
                            scores(i, c, k)
                            scores_for_max(i, c + 1, k)

            def rest_of(i, c, ffn=True):
                if c == 1 and isinstance(i, int):
                    pe.wait_ge(s_w, 32)
                    pe.wait_ge(s_bias, 7)
                    pe.wait_ge(s_ones, 2)
                    pe.wait_ge(s_kones, SLOTS)

                def maxima(*heads):
                    if has_next(i, c):
                        for k in heads:
                            scores_for_max(i, c + 1, k)

                def hidden(*units):
                    if ffn:
                        for u in units:
                            gemm1(i, c - c % 2 - 2, u)

                def second(n):
                    if ffn:
                        gemm2(i, c - 3, n)

                if c % 2 == 0:
                    scores(i, c, 4)
                    values(i, c, 0)
                    maxima(4)
                    scores(i, c, 5)
                    maxima(5)
                    scores(i, c, 6)
                    if c:
                        transpose_x(i, c - 1)
                    maxima(6)
                    scores(i, c, 7)
                    sums(i, c, 0)
                    maxima(7)
                    hidden(0, 1)
                    if has_next(i, c):
                        transpose_max(i, c + 1)
                    values(i, c, 1)
                    hidden(2, 3)
                    sums(i, c, 1)
                else:
                    hidden(4)
                    scores(i, c, 0)
                    hidden(5)
                    scores(i, c, 1)
                    hidden(6)
                    maxima(0, 1)
                    scores(i, c, 2)
                    hidden(7)
                    maxima(2)
                    scores(i, c, 3)
                    maxima(3)
                    second(0)
                    scores(i, c, 4)
                    maxima(4, 5)
                    transpose_x(i, c - 1)
                    maxima(6)
                    second(1)
                    scores(i, c, 5)
                    maxima(7)
                    values(i, c, 0)
                    scores(i, c, 6)
                    second(2)
                    if has_next(i, c):
                        transpose_max(i, c + 1)
                    scores(i, c, 7)
                    sums(i, c, 0)
                    second(3)
                    values(i, c, 1)
                    sums(i, c, 1)

            def tail():
                start(0, B)
                transpose_x(0, B - 1)
                for u in range(UNITS):
                    gemm1(0, B - 2, u)
                for n in range(8):
                    gemm2(0, B - 2 + n // 4, n % 4)

            half_steps(pe, start, rest_of, tail)


def kernel(x, ctx_2048, L0_xattn_gamma, L0_ffn_Wg, L0_ffn_W0a, L0_ffn_b0a, L0_ffn_W0b, L0_ffn_b0b,
           L0_ffn_W1a, L0_ffn_b1a, L0_ffn_W1b, L0_ffn_b1b):
    import concourse.bacc as bacc
    import numpy as np
    from concourse.bass_utils import run_bass_kernel_spmd

    f = np.ascontiguousarray
    ctx = np.asarray(ctx_2048)
    v = ctx.reshape(B, HEADS // 2, 2, DH, LC, 128).transpose(0, 5, 4, 1, 2, 3)
    vt_pad = np.zeros((B, 128, LC, HEADS // 2, 2, 32), ctx.dtype)
    for e in range(2):
        vt_pad[:, :, :, :, e, 16 * e:16 * e + 16] = v[:, :, :, :, e]
    w1 = np.stack([np.asarray(L0_ffn_W0a), np.asarray(L0_ffn_W1a)])
    w1 = w1.reshape(EXPERTS, HID, LC, 128).transpose(3, 2, 0, 1)
    w2 = np.stack([np.asarray(L0_ffn_W0b), np.asarray(L0_ffn_W1b)])
    w2 = w2.reshape(EXPERTS, L, HM, 128).transpose(3, 0, 2, 1)
    b1 = np.stack([np.asarray(L0_ffn_b0a), np.asarray(L0_ffn_b1a)]).reshape(UNITS, 128).T
    b2 = np.stack([np.asarray(L0_ffn_b0b), np.asarray(L0_ffn_b1b)])
    arrays = {
        "x": f(x), "ctx": f(ctx), "vt_pad": f(vt_pad.reshape(B, 128, -1)),
        "w1": f(w1.reshape(128, -1)), "w2": f(w2.reshape(128, -1)), "b1": f(b1),
        "b2": f(b2.reshape(-1)), "wg": f(np.asarray(L0_ffn_Wg).reshape(-1)),
        "gamma": f(np.asarray(L0_xattn_gamma).reshape(1)),
    }
    nc = bacc.Bacc("TRN2", target_bir_lowering=False, num_devices=1)
    args = [nc.dram_tensor(f"in_{n}", a.shape, F32, kind="ExternalInput").ap() for n, a in arrays.items()]
    out = nc.dram_tensor("out", (B, C, L), F32, kind="ExternalOutput").ap()
    build(nc, *args, out)
    r = run_bass_kernel_spmd(nc, [{f"in_{n}": a for n, a in arrays.items()}], core_ids=[0])
    return r.results[0]["out"]
```
